# Optimizing a Trainium2 kernel written in Bass

```python
import numpy as np
import jax
import jax.numpy as jnp

def _softmax(x, axis=-1):
    return jax.nn.softmax(x, axis=axis)

def _gelu(x):
    return jax.nn.gelu(x, approximate=True)

def _silu(x):
    return jax.nn.silu(x)

def _sigmoid(x):
    return jax.nn.sigmoid(x)

def _layernorm(x, axis=-1, eps=1e-05):
    m = jnp.mean(x, axis=axis, keepdims=True)
    v = jnp.var(x, axis=axis, keepdims=True)
    return (x - m) / jnp.sqrt(v + eps)

def _scatter_add(tgt, idx, src, axis=0):
    return tgt.at[idx].add(src)

def _segment_sum(src, seg, n):
    return jax.ops.segment_sum(src, seg, n)
kernel_name = 'mk_xattn_seq_d2_seqx_r4_8c29da'

def setup_inputs(seed: int=0):
    np.random.seed(seed)
    _w = jnp.asarray

    def _rec_inputs():
        import jax
        import jax.numpy as jnp
        _rk = jax.random.key(seed)
        x = -0.0001177 + 0.9999 * jax.random.normal(jax.random.fold_in(_rk, 1), (2, 512, 320), jnp.float32)
        _lenS = 512 - jax.random.randint(jax.random.fold_in(_rk, 7), (2,), 0, max(1, 512 // 4) + 1, jnp.int32)
        _lenS2 = 1024 - jax.random.randint(jax.random.fold_in(_rk, 8), (2,), 0, max(1, 1024 // 4) + 1, jnp.int32)
        _ctx_768P = jax.random.normal(jax.random.fold_in(_rk, 11), (2, 16, 192), jnp.float32)
        _ctx_768c = jax.random.dirichlet(jax.random.fold_in(_rk, 511), 0.3 * jnp.ones((16,), jnp.float32), (2, 1024))
        _ctx_768t = jnp.einsum('bsk,bkd->bsd', _ctx_768c, _ctx_768P)
        _ctx_768t = _ctx_768t * jax.lax.rsqrt(jnp.mean(jnp.square(_ctx_768t)) + 1e-12) * 0.953939
        ctx_768 = 0.00217967 + 0.999525 * (_ctx_768t + 0.3 * jax.random.normal(jax.random.fold_in(_rk, 611), (2, 1024, 192), jnp.float32))
        return (x, ctx_768)
    x, ctx_768 = _rec_inputs()

    def _L0_xattn_setup():
        import jax, jax.numpy as jnp
        import numpy as np
        B, S, DM, DC = (16, 1024, 320, 192)
        N_AOE, N_IMG, N_DELTA = (16, 16, 16)
        ANAT_GATE, DIS_GATE, DELTA_SCALE = (0.5, 0.5, 1.0)

        def _heads(x, h):
            b, s, d = x.shape
            return x.reshape(b, s, h, d // h).transpose(0, 2, 1, 3)

        def _attend(q, k, v, scale):
            scores = jnp.einsum('bhqd,bhkd->bhqk', q, k) * scale
            probs = jax.nn.softmax(scores, axis=-1)
            return jnp.einsum('bhqk,bhkd->bhqd', probs, v)
        key = jax.random.key(seed)
        ks = jax.random.split(key, 9)

        def lin(k, fan_in, fan_out):
            return jax.random.normal(k, (fan_in, fan_out), jnp.float32) / np.sqrt(fan_in)
        return {'hidden_states': jax.random.normal(ks[0], (B, S, DM), jnp.float32), 'encoder_hidden_states': jax.random.normal(ks[1], (B, N_AOE + N_IMG + N_DELTA, DC), jnp.float32), 'w_q': lin(ks[2], DM, DM), 'w_k': lin(ks[3], DC, DM), 'w_v': lin(ks[4], DC, DM), 'w_k_dis': lin(ks[5], DC, DM), 'w_v_dis': lin(ks[6], DC, DM), 'w_out': lin(ks[7], DM, DM), 'b_out': jnp.zeros((DM,), jnp.float32), 'n_heads': 8}
    _L0_xattn_all = _L0_xattn_setup()
    _L0_xattn_in = {k: v for k, v in _L0_xattn_all.items() if k in ('w_q', 'w_k', 'w_v', 'w_k_dis', 'w_v_dis', 'w_out', 'b_out')}
    del _L0_xattn_all

    def _L1_xattn_setup():
        import jax, jax.numpy as jnp
        import numpy as np
        HEADS = 20
        NUM_AOE = 16
        NUM_IP = 16
        key = jax.random.key(seed)
        ks = jax.random.split(key, 7)
        B, Sq, H = (8, 1024, 320)
        Skv, C = (109, 192)
        scale = 0.02
        return {'hidden_states': jax.random.normal(ks[0], (B, Sq, H), jnp.float32), 'encoder_hidden_states': jax.random.normal(ks[1], (B, Skv, C), jnp.float32), 'Wq': jax.random.normal(ks[2], (H, H), jnp.float32) * scale, 'Wk': jax.random.normal(ks[3], (C, H), jnp.float32) * scale, 'Wv': jax.random.normal(ks[4], (C, H), jnp.float32) * scale, 'Wo': jax.random.normal(ks[5], (H, H), jnp.float32) * scale, 'bo': jnp.zeros((H,), jnp.float32)}
    _L1_xattn_all = _L1_xattn_setup()
    _L1_xattn_in = {k: v for k, v in _L1_xattn_all.items() if k in ('Wq', 'Wk', 'Wv', 'Wo', 'bo')}
    del _L1_xattn_all
    return {'x': x, 'ctx_768': ctx_768, 'L0_xattn_w_q': _L0_xattn_in['w_q'], 'L0_xattn_w_k': _L0_xattn_in['w_k'], 'L0_xattn_w_v': _L0_xattn_in['w_v'], 'L0_xattn_w_k_dis': _L0_xattn_in['w_k_dis'], 'L0_xattn_w_v_dis': _L0_xattn_in['w_v_dis'], 'L0_xattn_w_out': _L0_xattn_in['w_out'], 'L0_xattn_b_out': _L0_xattn_in['b_out'], 'L1_xattn_Wq': _L1_xattn_in['Wq'], 'L1_xattn_Wk': _L1_xattn_in['Wk'], 'L1_xattn_Wv': _L1_xattn_in['Wv'], 'L1_xattn_Wo': _L1_xattn_in['Wo'], 'L1_xattn_bo': _L1_xattn_in['bo']}

def reference(x, ctx_768, L0_xattn_w_q, L0_xattn_w_k, L0_xattn_w_v, L0_xattn_w_k_dis, L0_xattn_w_v_dis, L0_xattn_w_out, L0_xattn_b_out, L1_xattn_Wq, L1_xattn_Wk, L1_xattn_Wv, L1_xattn_Wo, L1_xattn_bo):
    import jax
    import jax.numpy as jnp

    def _L0_xattn_ref(hidden_states, encoder_hidden_states, w_q, w_k, w_v, w_k_dis, w_v_dis, w_out, b_out, n_heads):
        import jax, jax.numpy as jnp
        import numpy as np
        B, S, DM, DC = (16, 1024, 320, 192)
        N_AOE, N_IMG, N_DELTA = (16, 16, 16)
        ANAT_GATE, DIS_GATE, DELTA_SCALE = (0.5, 0.5, 1.0)

        def _heads(x, h):
            b, s, d = x.shape
            return x.reshape(b, s, h, d // h).transpose(0, 2, 1, 3)

        def _attend(q, k, v, scale):
            scores = jnp.einsum('bhqd,bhkd->bhqk', q, k) * scale
            probs = jax.nn.softmax(scores, axis=-1)
            return jnp.einsum('bhqk,bhkd->bhqd', probs, v)
        residual = hidden_states
        dh = DM // n_heads
        scale = 1.0 / np.sqrt(dh)
        dis_tok = encoder_hidden_states[:, :N_AOE, :]
        anat_tok = encoder_hidden_states[:, N_AOE:N_AOE + N_IMG, :]
        delta_tok = encoder_hidden_states[:, -N_DELTA:, :]
        q = _heads(hidden_states @ w_q, n_heads)
        z_anat = _attend(q, _heads(anat_tok @ w_k, n_heads), _heads(anat_tok @ w_v, n_heads), scale)
        z_dis = _attend(q, _heads(dis_tok @ w_k_dis, n_heads), _heads(dis_tok @ w_v_dis, n_heads), scale)
        z_delta = _attend(q, _heads(delta_tok @ w_k_dis, n_heads), _heads(delta_tok @ w_v_dis, n_heads), scale)
        z = ANAT_GATE * z_anat + DIS_GATE * z_dis + DELTA_SCALE * z_delta
        out = z.transpose(0, 2, 1, 3).reshape(hidden_states.shape[0], -1, DM)
        out = out @ w_out + b_out
        return out + residual

    def _L1_xattn_ref(hidden_states, encoder_hidden_states, Wq, Wk, Wv, Wo, bo):
        import jax, jax.numpy as jnp
        import numpy as np
        HEADS = 20
        NUM_AOE = 16
        NUM_IP = 16
        B, Sq, H = hidden_states.shape
        Skv = encoder_hidden_states.shape[1]
        head_dim = H // HEADS
        residual = hidden_states
        q = (hidden_states @ Wq).reshape(B, Sq, HEADS, head_dim).transpose(0, 2, 1, 3)
        k = (encoder_hidden_states @ Wk).reshape(B, Skv, HEADS, head_dim).transpose(0, 2, 1, 3)
        v = (encoder_hidden_states @ Wv).reshape(B, Skv, HEADS, head_dim).transpose(0, 2, 1, 3)
        scores = jnp.einsum('bhqd,bhkd->bhqk', q, k) / jnp.sqrt(jnp.asarray(head_dim, q.dtype))
        probs = jax.nn.softmax(scores, axis=-1)
        scale_aoe = jnp.asarray(1.0, probs.dtype)
        scale_ip = jnp.asarray(1.0, probs.dtype)
        idx = jnp.arange(Skv)
        scale_vector = jnp.where(idx < NUM_AOE, scale_aoe, 1.0)
        scale_vector = jnp.where(idx >= Skv - NUM_IP, scale_vector * scale_ip, scale_vector)
        probs = probs * scale_vector
        probs = probs / probs.sum(axis=-1, keepdims=True)
        out = jnp.einsum('bhqk,bhkd->bhqd', probs, v)
        out = out.transpose(0, 2, 1, 3).reshape(B, Sq, H)
        out = out @ Wo + bo
        return out + residual
    x = _L0_xattn_ref(x, ctx_768, L0_xattn_w_q, L0_xattn_w_k, L0_xattn_w_v, L0_xattn_w_k_dis, L0_xattn_w_v_dis, L0_xattn_w_out, L0_xattn_b_out, 8)
    x = _L1_xattn_ref(x, ctx_768, L1_xattn_Wq, L1_xattn_Wk, L1_xattn_Wv, L1_xattn_Wo, L1_xattn_bo)
    return x

_drawn_inputs = setup_inputs


def setup_inputs(seed=0):
    import zlib

    import numpy as np

    out = dict(_drawn_inputs(seed))
    spreads = {'L0_xattn_b_out': (0.0, 0.1), 'L1_xattn_bo': (0.0, 0.1)}
    factors = {'L1_xattn_Wq': 8.0, 'L1_xattn_Wk': 8.0}
    for name, (base, spread) in spreads.items():
        noise = np.random.default_rng([zlib.crc32(name.encode()), seed]).standard_normal(out[name].shape)
        drawn = base * np.exp(spread * noise) if base else spread * noise
        out[name] = jnp.asarray(drawn.astype(out[name].dtype))
    for name, factor in factors.items():
        out[name] = (out[name] * factor).astype(out[name].dtype)
    return out
```

```python
import concourse.bass as bass
import numpy as np
from concourse import mybir
from contextlib import ExitStack

ALU = mybir.AluOpType
ACT = mybir.ActivationFunctionType
AX = mybir.AxisListType
F32 = mybir.dt.float32
BF16 = mybir.dt.bfloat16


def two_layer_cross_attention(nc, x, ctx_768, w_q0, w_k0, w_v0, w_kd0, w_vd0, w_out0, b_out0,
                              w_q1, w_k1, w_v1, w_o1, b_o1, out):
    B, SQ, DM = x.shape
    SK, DC = ctx_768.shape[1:]
    P = 128
    NT = B * SQ // P
    TB = NT // B
    NKT = SK // P
    H0, D0, NS, TOK = 8, 40, 3, 16
    KEY0 = NS * TOK
    COL0 = H0 * KEY0
    H1, D1, GH = 20, 16, 4
    GW = GH * D1
    GB = H1 // GH
    NG = B * GB
    CH = [(0, 128), (128, 128), (256, 64)]
    CC = [(0, 128), (128, 64)]
    HC = [(0, 3), (3, 3), (6, 2)]
    NPAIR = [(0, 0), (0, 1), (0, 2), (1, 0), (1, 1), (2, 0)]
    STK = len(NPAIR) * D1
    BUF = 3
    LEAD = 8
    UNITS = GH * TB * 2
    PER = UNITS // NKT

    k_parts = nc.dram_tensor("k_parts", [3, B * DM, SK], BF16, kind="Internal").ap()
    q_parts = nc.dram_tensor("q_parts", [3, B * DM, SQ], BF16, kind="Internal").ap()

    with ExitStack() as ctx:
        def sb(name, shape, dt=F32):
            return ctx.enter_context(nc.sbuf_tensor(name, shape, dt))

        def sem(name):
            return ctx.enter_context(nc.semaphore(name))

        ident_f = sb("ident_f", [P, P])
        ident_b = sb("ident_b", [P, P], BF16)
        xs = sb("xs", [P, NT, DM])
        cs = sb("cs", [P, B * NKT, DC])
        attn = cs[:, :, :].rearrange("p t n -> p (t n)")[:, 0:NG * TB * GW].rearrange(
            "p (q g n) -> p q g n", g=NG, q=TB)
        xT = sb("xT", [P, 3, B * SQ])
        cT = sb("cT", [P, 2, B * SK])
        wq0 = sb("wq0", [P, 3, DM])
        wk0 = sb("wk0", [P, 2, DM])
        wv0 = sb("wv0", [P, 2, DM])
        wkd0 = sb("wkd0", [P, 2, DM])
        wvd0 = sb("wvd0", [P, 2, DM])
        wout0 = sb("wout0", [P, 3, DM])
        wq1 = sb("wq1", [P, 3, DM])
        wk1 = sb("wk1", [P, 2, DM])
        wv1 = sb("wv1", [P, 2, DM])
        wo1 = sb("wo1", [P, 3, DM])
        bias0 = sb("bias0", [P, DM])
        bias1 = sb("bias1", [P, DM])
        mask_k = sb("mask_k", [P, 3 * KEY0])
        mask_v = sb("mask_v", [P, 3 * KEY0])
        U = sb("U", [P, B, 3, DM])
        d0 = sb("d0", [P, 2, COL0])
        max0 = sb("max0", [P, 2, H0 * NS])
        sum0 = sb("sum0", [P, 2, H0 * NS])
        rec0 = sb("rec0", [P, 2, H0 * NS])
        parts = sb("parts", [P, 2, 3, 512], BF16)
        rest = sb("rest", [P, 2, 512])
        KS = sb("KS", [P, BUF, GH, SK], BF16)
        QS = sb("QS", [P, BUF, GH, SQ], BF16)
        q0T = QS[:, :, :, :].rearrange("p a b c -> p (a b c)").bitcast(F32).rearrange(
            "p (c t) -> p c t", c=3)
        V = sb("V", [P, NG, NKT, GW])
        VS = sb("VS", [P, BUF, NKT, GH, 2 * D1])
        probs = sb("probs", [P, 4, 2, SQ])
        pr = probs[:, :, :, :].rearrange("p a b c -> p (a b c)")
        nk, nv = 3 * B * 3 * KEY0, 3 * B * COL0
        k0bd = pr[:, 0:nk].rearrange("p (c b n) -> p c b n", c=3, b=B)
        v0bd = pr[:, nk:nk + nv].rearrange("p (c b n) -> p c b n", c=3, b=B)
        pT = pr[:, nk + nv:nk + nv + 2 * COL0].rearrange("p (r n) -> p r n", r=2)
        o_raw = sb("o_raw", [P, SQ])
        o_rec = sb("o_rec", [P, TB * GH])
        mx = sb("mx", [P, BUF, UNITS])
        neg = sb("neg", [P, TB * GH])
        neg_r = sb("neg_r", [P, TB * GH])
        one = sb("one", [P, TB * GH])
        neg_p = sb("neg_p", [P, 3, GH, TB], BF16)
        mT = sb("mT", [3 * GH, SQ], BF16)
        oT = sb("oT", [P, 2, 3, P])
        ps = ctx.enter_context(nc.psum_tensor("ps", [P, 8, 512], F32))
        ps7b = ps[:, 7, :].bitcast(BF16)

        x_in = [sem(f"x_in{b}") for b in range(B)]
        c_in = [sem(f"c_in{b}") for b in range(B)]
        wq0_in, wk0_in, wout0_in = sem("wq0_in"), sem("wk0_in"), sem("wout0_in")
        wq1_in, wkv1_in, wo1_in, bias_in = sem("wq1_in"), sem("wkv1_in"), sem("wo1_in"), sem("bias_in")
        id_step, id_ready, mask_step, mask_ready = sem("id_step"), sem("id_ready"), sem("mask_step"), sem("mask_ready")
        zero_ready, ones_ready = sem("zero_ready"), sem("ones_ready")
        xT_mm, xT_copied = sem("xT_mm"), sem("xT_copied")
        cT_mm, cT_copied = sem("cT_mm"), sem("cT_copied")
        q0_mm, q0_copied = sem("q0_mm"), sem("q0_copied")
        kv0_mm, k0bd_made, v0bd_made = sem("kv0_mm"), sem("k0bd_made"), sem("v0bd_made")
        u_mm, u_copied = sem("u_mm"), sem("u_copied")
        s0_mm, max0_done, sub0_done = sem("s0_mm"), sem("max0_done"), sem("sub0_done")
        exp0_done, sum0_done, rec0_done, norm0_done = sem("exp0_done"), sem("sum0_done"), sem("rec0_done"), sem("norm0_done")
        pT_mm, pT_copied = sem("pT_mm"), sem("pT_copied")
        xb_done, x1_mm, x1_added = sem("xb_done"), sem("x1_mm"), sem("x1_added")
        x1T_mm, x1T_copied, x1b_done = sem("x1T_mm"), sem("x1T_copied"), sem("x1b_done")
        proj_mm, v_copied = sem("proj_mm"), sem("v_copied")
        hi_done, rest_done, mid_done, lo_done = sem("hi_done"), sem("rest_done"), sem("mid_done"), sem("lo_done")
        stored = [sem(f"stored{k}") for k in range(16)]
        stack_in = [sem(f"stack_in{j}") for j in range(BUF)]
        v_staged, max_mm, max_done = sem("v_staged"), sem("max_mm"), sem("max_done")
        neg_made, neg_step, neg_done, mT_mm, mT_copied, m_in = sem("neg_made"), sem("neg_step"), sem("neg_done"), sem("mT_mm"), sem("mT_copied"), sem("m_in")
        s_mm, exp_done, pv_mm = sem("s_mm"), sem("exp_done"), sem("pv_mm")
        o_copied, oT_mm, o_rec_done, o_norm = sem("o_copied"), sem("oT_mm"), sem("o_rec_done"), sem("o_norm")
        fT_mm, fT_copied, fin_mm, fin_added, out_done = sem("fT_mm"), sem("fT_copied"), sem("fin_mm"), sem("fin_added"), sem("out_done")

        k_units = [[("k", b, c, h) for c in (0, 1) for h in range(2)] + [("k", b, 2, 0)] for b in range(B)]
        v_units = [[("v", b, t) for t in range(NKT)] for b in range(B)]
        q_units = [[("q", b, c) for c in range(3)] for b in range(B)]
        row = k_units[0] + v_units[0] + k_units[1] + v_units[1]
        STEPS = NT + 5
        plan = [row[0:3], row[3:6], row[6:8], row[8:10], row[10:12], row[12:14], row[14:16], row[16:18],
                q_units[0] + row[18:19], row[19:21], row[21:23], row[23:26], q_units[1]]
        assert len(plan) == STEPS
        order = [u for step in plan for u in step]
        split_no = {u: k for k, u in enumerate(u for u in order if u[0] != "v")}
        PROJ = (5, 6, 7)

        def stores_of(u):
            return 2 if u[0] == "k" and u[2] == 2 else 1

        def split_rows(u):
            return CH[u[2]][1] if u[0] == "q" or u[2] < 2 else P

        block = ctx.enter_context(nc.Block())

        def group_index(g):
            return g if isinstance(g, int) else g.with_bounds(min_val=0, max_val=NG - 1)

        def by_rows(w, chunks):
            return [(c, n, w[r:r + n, :]) for c, (r, n) in enumerate(chunks)]

        @block.sync
        def _(sp):
            def weight(dst, w, chunks, s):
                for c, n, src in by_rows(w, chunks):
                    sp.dma_start(dst[0:n, c, :], src).then_inc(s, 16)

            xv = x.rearrange("b (t p) n -> b p t n", p=P)
            sp.dma_start(xs[:, 0:TB, :], xv[0]).then_inc(x_in[0], 16)
            weight(wq0, w_q0, CH, wq0_in)
            sp.dma_start(xs[:, TB:NT, :], xv[1]).then_inc(x_in[1], 16)
            weight(wout0, w_out0, [(HC[c][0] * D0, HC[c][1] * D0) for c in range(3)], wout0_in)
            for dst, b in ((bias0, b_out0), (bias1, b_o1)):
                sp.dma_start(dst[:, :], b.partition_broadcast(P)).then_inc(bias_in, 16)
            weight(wq1, w_q1, CH, wq1_in)
            weight(wo1, w_o1, CH, wo1_in)

            def store(u):
                k = split_no[u]
                sp.wait_ge(lo_done, k + 1)
                r = k % 2
                if u[0] == "q":
                    r0, n = CH[u[2]]
                    dst = q_parts[:, u[1] * DM + r0:u[1] * DM + r0 + n, :].rearrange("a r n -> r a n")
                    sp.dma_start(dst, parts[0:n, r, :, :]).then_inc(stored[k], 16)
                elif u[2] < 2:
                    r0, n = CH[u[2]]
                    dst = k_parts[:, u[1] * DM + r0:u[1] * DM + r0 + n, u[3] * 512:u[3] * 512 + 512].rearrange("a r n -> r a n")
                    sp.dma_start(dst, parts[0:n, r, :, :]).then_inc(stored[k], 16)
                else:
                    r0, n = CH[2]
                    for h in range(2):
                        dst = k_parts[:, u[1] * DM + r0:u[1] * DM + r0 + n, h * 512:h * 512 + 512].rearrange("a r n -> r a n")
                        sp.dma_start(dst, parts[n * h:n * h + n, r, :, :]).then_inc(stored[k], 16)

            def load(g, j):
                for n, (pq, pk) in enumerate(NPAIR):
                    kv = k_parts[pk, bass.ds(group_index(g) * GW, GW), :].rearrange("(h d) n -> d h n", d=D1)
                    qv = q_parts[pq, bass.ds(group_index(g) * GW, GW), :].rearrange("(h d) n -> d h n", d=D1)
                    sp.dma_start(KS[n * D1:n * D1 + D1, j, :, :], kv).then_inc(stack_in[j], 16)
                    sp.dma_start(QS[n * D1:n * D1 + D1, j, :, :], qv).then_inc(stack_in[j], 16)

            def scratch_written(b):
                for u in k_units[b] + q_units[b]:
                    sp.wait_ge(stored[split_no[u]], 16 * stores_of(u))

            for u in (u for step in plan[:NT + 1] for u in step if u[0] != "v"):
                store(u)
            scratch_written(0)
            sp.wait_ge(s0_mm, NT)
            load(0, 0)
            load(1, 1)
            for u in (u for step in plan[NT + 1:] for u in step if u[0] != "v"):
                store(u)
            scratch_written(1)

            def max_rows(g, j):
                sp.wait_ge(mT_copied, g + 1)
                sp.dma_start(QS[STK:STK + 3, j, :, :], mT[:, :]).then_inc(m_in, 16)

            max_rows(0, 0)
            with sp.Fori(0, NG // BUF) as i:
                for j in range(BUF):
                    g = i * BUF + j
                    if j < BUF - 1:
                        sp.wait_ge(s_mm, g * 16 + 1)
                        load(g + 2, (j + 2) % BUF)
                    else:
                        with sp.If(i < NG // BUF - 1):
                            sp.wait_ge(s_mm, g * 16 + 1)
                            load(g + 2, (j + 2) % BUF)
                    max_rows(g + 1, (j + 1) % BUF)
            for t in range(NT):
                sp.wait_ge(fin_added, t + 1)
                sp.dma_start(out.rearrange("b (t p) n -> (b t) p n", p=P)[t], xs[:, t, :]).then_inc(out_done, 16)
            sp.wait_ge(out_done, 16 * NT)

        @block.gpsimd
        def _(pool):
            def diagonal(m, done):
                pool.affine_select(out=m, in_=m, compare_op=ALU.not_equal, fill=1.0, base=0,
                                   pattern=[[-1, P]], channel_multiplier=1).then_inc(done, 1)

            pool.memset(ident_f[:, :], 0.0).then_inc(id_step, 1)
            pool.memset(ident_b[:, :], 0.0).then_inc(id_step, 1)
            pool.memset(mask_k[:, :], 1.0).then_inc(mask_step, 1)
            pool.wait_ge(id_step, 2)
            diagonal(ident_f[:, :], id_ready)
            diagonal(ident_b[:, :], id_ready)
            mk = mask_k[:, :].rearrange("p (h k) -> p h k", h=3)
            mv = mask_v[:, :].rearrange("p (h k) -> p h k", h=3)
            pool.wait_ge(mask_step, 1)
            pool.affine_select(out=mk, in_=mk, compare_op=ALU.is_ge, fill=0.0, base=0,
                               pattern=[[-D0, 3], [0, KEY0]], channel_multiplier=1).then_inc(mask_step, 1)
            pool.wait_ge(mask_step, 2)
            pool.affine_select(out=mk, in_=mk, compare_op=ALU.is_ge, fill=0.0, base=D0 - 1,
                               pattern=[[D0, 3], [0, KEY0]], channel_multiplier=-1).then_inc(mask_step, 1)
            pool.wait_ge(mask_step, 3)
            pool.tensor_scalar(mv[:, :, 0:2 * TOK], mk[:, :, 0:2 * TOK], 0.5, None, ALU.mult).then_inc(mask_ready, 1)
            pool.tensor_scalar(mv[:, :, 2 * TOK:KEY0], mk[:, :, 2 * TOK:KEY0], 1.0, None, ALU.mult).then_inc(mask_ready, 1)
            pool.memset(v0bd, 0.0).then_inc(zero_ready, 1)
            pair_of_ones = float(np.array([0x3F803F80], np.uint32).view(np.float32)[0])
            pool.wait_ge(mask_ready, 2)
            pool.wait_ge(zero_ready, 1)
            pool.memset(KS[STK:STK + 3, :, :, :].rearrange("p a b c -> p (a b c)").bitcast(F32), pair_of_ones).then_inc(ones_ready, 1)
            pool.wait_ge(ones_ready, 1)
            pool.memset(VS[:, :, :, :, :], 1.0).then_inc(ones_ready, 1)
            pool.memset(one[:, :], 1.0).then_inc(ones_ready, 1)
            for b in range(B):
                pool.wait_ge(x_in[b], 16)
                pool.wait_ge(xT_mm, 3 * b + 3)
                pool.wait_ge(bias_in, 32)
                xb = xs[:, b * TB:(b + 1) * TB, :]
                pool.tensor_tensor(xb, xb, bias0[:, :].unsqueeze(1).to_broadcast([P, TB, DM]), ALU.add).then_inc(xb_done, 1)
            for s in range(STEPS):
                if 1 <= s <= NT:
                    t = s - 1
                    pool.wait_ge(rec0_done, t + 1)
                    e = d0[:, t % 2, :].rearrange("p (g k) -> p g k", k=TOK)
                    rb = rec0[:, t % 2, :].unsqueeze(2).to_broadcast([P, H0 * NS, TOK])
                    pool.tensor_tensor(e, e, rb, ALU.mult).then_inc(norm0_done, 1)
                if 4 <= s < NT + 4:
                    t = s - 4
                    pool.wait_ge(x1T_mm, t + 1)
                    pool.tensor_tensor(xs[:, t, :], xs[:, t, :], bias1[:, :], ALU.add).then_inc(x1b_done, 1)
                for u in plan[s]:
                    if u[0] == "v":
                        continue
                    k = split_no[u]
                    n = split_rows(u)
                    pool.wait_ge(rest_done, k + 1)
                    pool.tensor_copy(parts[0:n, k % 2, 1, :], rest[0:n, k % 2, :]).then_inc(mid_done, 1)
                    pool.wait_ge(mid_done, k + 1)
                    pool.tensor_tensor(parts[0:n, k % 2, 2, :], rest[0:n, k % 2, :], parts[0:n, k % 2, 1, :],
                                       ALU.subtract).then_inc(lo_done, 1)

            def stage_v(g, j):
                src = V[:, bass.ds(group_index(g), 1), :, :].rearrange("p o k (h d) -> p (o k) h d", h=GH)
                pool.wait_ge(v_copied, B * NKT)
                pool.tensor_copy(VS[:, j, :, :, 0:D1], src).then_inc(v_staged, 1)

            def neg_parts(g):
                pool.wait_ge(neg_made, g + 1)
                pool.wait_ge(mT_mm, g)
                pv = [neg_p[:, a, :, :].rearrange("p h q -> p (h q)") for a in range(3)]
                pool.tensor_tensor(pv[0], neg[:, :], one[:, :], ALU.mult).then_inc(neg_step, 1)
                pool.wait_ge(neg_step, g * 3 + 1)
                pool.tensor_tensor(neg_r[:, :], neg[:, :], pv[0], ALU.subtract).then_inc(neg_step, 1)
                pool.wait_ge(neg_step, g * 3 + 2)
                pool.tensor_tensor(pv[1], neg_r[:, :], one[:, :], ALU.mult).then_inc(neg_step, 1)
                pool.wait_ge(neg_step, g * 3 + 3)
                pool.tensor_tensor(pv[2], neg_r[:, :], pv[1], ALU.subtract).then_inc(neg_done, 1)

            pool.wait_ge(ones_ready, 3)
            stage_v(0, 0)
            neg_parts(0)
            with pool.Fori(0, NG // BUF) as i:
                for j in range(BUF):
                    g = i * BUF + j
                    pool.wait_ge(s_mm, g * 16 + 1)
                    stage_v(g + 1, (j + 1) % BUF)
                    neg_parts(g + 1)

        @block.scalar
        def _(act):
            def weight(dst, w, chunks, s):
                for c, n, src in by_rows(w, chunks):
                    act.dma_start(dst[0:n, c, :], src).then_inc(s, 16)

            cv = ctx_768.rearrange("b (t p) n -> b p t n", p=P)
            act.dma_start(cs[:, 0:NKT, :], cv[0]).then_inc(c_in[0], 16)
            act.dma_start(cs[:, NKT:2 * NKT, :], cv[1]).then_inc(c_in[1], 16)
            for dst, w in ((wk0, w_k0), (wkd0, w_kd0), (wv0, w_v0), (wvd0, w_vd0)):
                weight(dst, w, CC, wk0_in)
            for dst, w in ((wk1, w_k1), (wv1, w_v1)):
                weight(dst, w, CC, wkv1_in)
            for w in range(3 * B):
                b, c = w // 3, w % 3
                n = HC[c][1] * D0
                act.wait_ge(q0_mm, w + 1)
                act.copy(q0T[0:n, c, b * SQ:(b + 1) * SQ], ps[0:n, (6 + w) % 4, :]).then_inc(q0_copied, 1)
            for v in range(8):
                qd, c = v // 2, v % 2
                n = CC[c][1]
                act.wait_ge(cT_mm, v + 1)
                act.copy(cT[0:n, c, qd * 512:qd * 512 + 512], ps[0:n, 4 + v % 4, :]).then_inc(cT_copied, 1)
            for y in range(3 * B):
                b, k = y // 3, y % 3
                act.wait_ge(u_mm, y + 1)
                act.copy(U[:, b, k, :], ps[:, 6 + y % 2, 0:DM]).then_inc(u_copied, 1)

            f = 0
            for s in range(STEPS):
                if s < NT:
                    act.wait_ge(sub0_done, s + 1)
                    act.activation(d0[:, s % 2, :], d0[:, s % 2, :], ACT.Exp, scale=float(D0) ** -0.5).then_inc(exp0_done, 1)
                if 2 <= s < NT + 2:
                    t = s - 2
                    act.wait_ge(pT_mm, t + 1)
                    if t >= 2:
                        act.wait_ge(x1_mm, t - 1)
                    act.copy(pT[:, t % 2, :], ps[:, 2, 0:COL0]).then_inc(pT_copied, 1)
                if 4 <= s < NT + 4:
                    t = s - 4
                    act.wait_ge(x1T_mm, t + 1)
                    act.copy(xT[:, 0:2, t * P:(t + 1) * P], ps[:, 4, 0:2 * P].rearrange("p (c n) -> p c n", c=2)).then_inc(x1T_copied, 1)
                    act.copy(xT[0:64, 2, t * P:(t + 1) * P], ps[0:64, 4, 2 * P:3 * P]).then_inc(x1T_copied, 1)
                for u in plan[s]:
                    if u[0] != "v":
                        k = split_no[u]
                        n = split_rows(u)
                        act.wait_ge(proj_mm, f + 1)
                        if k >= 2:
                            old = [w for w in split_no if split_no[w] == k - 2][0]
                            act.wait_ge(stored[k - 2], 16 * stores_of(old))
                        act.copy(parts[0:n, k % 2, 0, :], ps[0:n, PROJ[f % 3], :]).then_inc(hi_done, 1)
                    f += 1

            def mT_copy(g):
                act.wait_ge(mT_mm, g + 1)
                act.wait_ge(m_in, g * 16)
                act.copy(mT[:, :], ps7b[0:3 * GH, 0:SQ]).then_inc(mT_copied, 1)

            def exp_pair(g, kt, p):
                n = g * 16 + (2 * kt + p)
                act.wait_ge(s_mm, n + 1)
                if kt >= 2:
                    act.wait_ge(pv_mm, g * NKT + (kt - 1))
                act.activation(probs[:, (2 * kt + p) % 4, :, :], ps[:, 2 + 2 * p:4 + 2 * p, :], ACT.Exp,
                               scale=float(D1) ** -0.5).then_inc(exp_done, 1)

            def copy_o(g):
                act.wait_ge(pv_mm, g * NKT + NKT)
                act.copy(o_raw[:, :], ps[:, 6, :]).then_inc(o_copied, 1)

            def copy_final(t):
                act.wait_ge(fT_mm, t + 1)
                if t >= 2:
                    act.wait_ge(fin_mm, t - 1)
                bk = 0 if t < TB else 2 + t % 2
                act.copy(oT[:, t % 2, 0:2, :], ps[:, bk, 0:2 * P].rearrange("p (c n) -> p c n", c=2)).then_inc(fT_copied, 1)
                act.copy(oT[0:64, t % 2, 2, :], ps[0:64, bk, 2 * P:3 * P]).then_inc(fT_copied, 1)

            def group(g, j, i, last):
                for kt in range(NKT):
                    if kt == 0:
                        if j > 0 or last:
                            copy_o(g - 1)
                        else:
                            with act.If(i > 0):
                                copy_o(g - 1)
                    if kt < NKT - 1:
                        exp_pair(g, kt + 1, 0)
                        exp_pair(g, kt + 1, 1)
                    elif not last:
                        for p in range(2):
                            n = g * 16 + 16 + p
                            act.wait_ge(s_mm, n + 1)
                            act.wait_ge(pv_mm, g * NKT + (NKT - 1))
                            act.activation(probs[:, p, :, :], ps[:, 2 + 2 * p:4 + 2 * p, :], ACT.Exp,
                                           scale=float(D1) ** -0.5).then_inc(exp_done, 1)
                    if kt == NKT - 2 and not last:
                        mT_copy(g + 1)
                    if last and kt % 2 == 0:
                        copy_final(kt // 2)

            mT_copy(0)
            exp_pair(0, 0, 0)
            exp_pair(0, 0, 1)
            with act.Fori(0, NG // BUF) as i:
                for j in range(BUF):
                    group(i * BUF + j, j, i, False)
            group(NG - 1, 0, None, True)
            copy_o(NG - 1)
            for t in range(TB, NT):
                copy_final(t)

        @block.vector
        def _(dve):
            for u in range(3 * B):
                b, c = u // 3, u % 3
                n = CH[c][1]
                dve.wait_ge(xT_mm, u + 1)
                dve.tensor_copy(xT[0:n, c, b * SQ:(b + 1) * SQ], ps[0:n, u % 4, :]).then_inc(xT_copied, 1)
            dve.wait_ge(mask_ready, 2)
            for kv, (bank, made, mask) in enumerate(((4, k0bd_made, mask_k), (5, v0bd_made, mask_v))):
                dve.wait_ge(kv0_mm, kv + 1)
                if kv:
                    dve.wait_ge(zero_ready, 1)
                for c, (h0, nh) in enumerate(HC):
                    n = nh * D0
                    src = ps[0:n, bank, c * B * KEY0:(c + 1) * B * KEY0].rearrange("p (b k) -> p b k", b=B)
                    dst = v0bd[0:n, c, :, h0 * KEY0:(h0 + nh) * KEY0] if kv else k0bd[0:n, c, :, 0:nh * KEY0]
                    dve.tensor_tensor(dst.rearrange("p b (h k) -> p b h k", h=nh),
                                      src.unsqueeze(2).to_broadcast([n, B, nh, KEY0]),
                                      mask[0:n, 0:nh * KEY0].rearrange("p (h k) -> p h k", h=nh).unsqueeze(1).to_broadcast([n, B, nh, KEY0]),
                                      ALU.mult).then_inc(made, 1)

            f = 0
            for s in range(STEPS):
                if s < NT:
                    sc = ps[:, s % 2, 0:COL0].rearrange("p (g k) -> p g k", k=TOK)
                    dve.wait_ge(s0_mm, s + 1)
                    dve.tensor_reduce(max0[:, s % 2, :], sc, AX.X, ALU.max).then_inc(max0_done, 1)
                    dve.wait_ge(max0_done, s + 1)
                    if s >= 2:
                        dve.wait_ge(pT_mm, s - 1)
                    dve.tensor_tensor(d0[:, s % 2, :].rearrange("p (g k) -> p g k", k=TOK), sc,
                                      max0[:, s % 2, :].unsqueeze(2).to_broadcast([P, H0 * NS, TOK]),
                                      ALU.subtract).then_inc(sub0_done, 1)
                if 1 <= s <= NT:
                    t = s - 1
                    dve.wait_ge(exp0_done, t + 1)
                    dve.tensor_reduce(sum0[:, t % 2, :], d0[:, t % 2, :].rearrange("p (g k) -> p g k", k=TOK),
                                      AX.X, ALU.add).then_inc(sum0_done, 1)
                    dve.wait_ge(sum0_done, t + 1)
                    if t >= 2:
                        dve.wait_ge(norm0_done, t - 1)
                    dve.reciprocal(rec0[:, t % 2, :], sum0[:, t % 2, :]).then_inc(rec0_done, 1)
                if 3 <= s < NT + 3:
                    t = s - 3
                    dve.wait_ge(x1_mm, t + 1)
                    dve.wait_ge(xb_done, t // TB + 1)
                    dve.tensor_tensor(xs[:, t, :], ps[:, 3, 0:DM], xs[:, t, :], ALU.add).then_inc(x1_added, 1)
                for u in plan[s]:
                    bank = PROJ[f % 3]
                    dve.wait_ge(proj_mm, f + 1)
                    if u[0] == "v":
                        g0 = u[1] * GB
                        dve.tensor_copy(V[:, g0:g0 + GB, u[2], :], ps[:, bank, 0:DM].rearrange("p (g n) -> p g n", g=GB)).then_inc(v_copied, 1)
                    else:
                        k = split_no[u]
                        n = split_rows(u)
                        dve.wait_ge(hi_done, k + 1)
                        if k >= 2:
                            dve.wait_ge(lo_done, k - 1)
                        dve.tensor_tensor(rest[0:n, k % 2, :], ps[0:n, bank, :], parts[0:n, k % 2, 0, :],
                                          ALU.subtract).then_inc(rest_done, 1)
                    f += 1

            def maximum(g, j, u):
                n = g * UNITS + u
                dve.wait_ge(max_mm, n + 1)
                dve.tensor_reduce(mx[:, j, u:u + 1], ps[:, u % 2, :], AX.X, ALU.max).then_inc(max_done, 1)

            def negate(g, j):
                dve.wait_ge(max_done, g * UNITS + UNITS)
                dve.wait_ge(neg_done, g)
                dve.tensor_reduce(neg[:, :], mx[:, j, :].rearrange("p (m h) -> p m h", h=2), AX.X, ALU.max,
                                  negate=True).then_inc(neg_made, 1)

            def norm_o(g):
                o = ps[:, 7, :].rearrange("p (m c) -> p m c", c=2 * D1)
                dve.wait_ge(oT_mm, g + 1)
                dve.reciprocal(o_rec[:, :], o[:, :, D1]).then_inc(o_rec_done, 1)
                dve.wait_ge(o_rec_done, g + 1)
                dst = attn[:, :, bass.ds(group_index(g), 1), :].rearrange("p q o (h d) -> p q (o h) d", d=D1)
                dve.tensor_tensor(dst, o[:, :, 0:D1].rearrange("p (q h) d -> p q h d", q=TB),
                                  o_rec[:, :].rearrange("p (q h) -> p q h", q=TB).unsqueeze(3).to_broadcast([P, TB, GH, D1]), ALU.mult).then_inc(o_norm, 1)

            def group(g, j, i, last):
                for kt in range(NKT):
                    if kt == 1:
                        if j > 0 or last:
                            norm_o(g - 1)
                        else:
                            with dve.If(i > 0):
                                norm_o(g - 1)
                    if last:
                        continue
                    if kt < NKT - 2:
                        for u in range(LEAD + PER * kt, LEAD + PER * kt + PER):
                            maximum(g + 1, (j + 1) % BUF, u)
                        if kt == NKT - 3:
                            negate(g + 1, (j + 1) % BUF)
                    elif j < BUF - 1:
                        for u in range(PER * (kt - NKT + 2), PER * (kt - NKT + 3)):
                            maximum(g + 2, (j + 2) % BUF, u)
                    else:
                        with dve.If(i < NG // BUF - 1):
                            for u in range(PER * (kt - NKT + 2), PER * (kt - NKT + 3)):
                                maximum(g + 2, (j + 2) % BUF, u)

            for u in range(UNITS):
                maximum(0, 0, u)
            negate(0, 0)
            for u in range(LEAD):
                maximum(1, 1, u)
            with dve.Fori(0, NG // BUF) as i:
                for j in range(BUF):
                    group(i * BUF + j, j, i, False)

            def final(t):
                dve.wait_ge(fin_mm, t + 1)
                dve.wait_ge(x1b_done, t + 1)
                bk = 1 if t < TB else 4 + t % 2
                dve.tensor_tensor(xs[:, t, :], ps[:, bk, 0:DM], xs[:, t, :], ALU.add).then_inc(fin_added, 1)

            group(NG - 1, 0, None, True)
            for t in range(TB):
                final(t)
            norm_o(NG - 1)
            for t in range(TB, NT):
                final(t)

        @block.tensor
        def _(pe):
            def mm_chain(dst, pairs, s=None):
                for n, (l, r) in enumerate(pairs):
                    m = pe.matmul(dst, l, r, start=(n == 0), stop=(n == len(pairs) - 1))
                if s is not None:
                    m.then_inc(s, 1)
                return m

            pe.wait_ge(id_ready, 1)
            for u in range(3 * B):
                b, c = u // 3, u % 3
                r0, n = CH[c]
                pe.wait_ge(x_in[b], 16)
                if u >= 4:
                    pe.wait_ge(xT_copied, u - 3)
                for k in range(TB):
                    m = pe.transpose(ps[0:n, u % 4, k * P:(k + 1) * P], xs[:, b * TB + k, r0:r0 + n], ident_f[:, :])
                m.then_inc(xT_mm, 1)
            pe.wait_ge(wq0_in, 16 * 3)
            pe.wait_ge(xT_copied, 3 * B)
            for w in range(3 * B):
                b, c = w // 3, w % 3
                h0, nh = HC[c]
                if w >= 4:
                    pe.wait_ge(q0_copied, w - 3)
                mm_chain(ps[0:nh * D0, (6 + w) % 4, :],
                         [(wq0[0:n, k, h0 * D0:(h0 + nh) * D0], xT[0:n, k, b * SQ:(b + 1) * SQ]) for k, (_, n) in enumerate(CH)], q0_mm)
            for v in range(8):
                qd, c = v // 2, v % 2
                r0, n = CC[c]
                pe.wait_ge(c_in[qd // 2], 16)
                if v >= 4:
                    pe.wait_ge(cT_copied, v - 3)
                for k in range(4):
                    m = pe.transpose(ps[0:n, 4 + v % 4, k * P:(k + 1) * P], cs[:, qd * 4 + k, r0:r0 + n], ident_f[:, :])
                m.then_inc(cT_mm, 1)
            pe.wait_ge(cT_copied, 8)
            pe.wait_ge(wk0_in, 16 * 8)
            for kv, (dis, anat) in enumerate(((wkd0, wk0), (wvd0, wv0))):
                for c, (h0, nh) in enumerate(HC):
                    dst = ps[0:nh * D0, 4 + kv, c * B * KEY0:(c + 1) * B * KEY0].rearrange("p (b s k) -> p b s k", b=B, s=NS)
                    for st, (w, t0) in enumerate(((dis, 0), (anat, TOK), (dis, SK - TOK))):
                        m = mm_chain(dst[:, :, st, :],
                                     [(w[0:n, k, h0 * D0:(h0 + nh) * D0],
                                       cT[0:n, k, :].rearrange("p (b n) -> p b n", b=B)[:, :, t0:t0 + TOK]) for k, (_, n) in enumerate(CC)])
                m.then_inc(kv0_mm, 1)
            pe.wait_ge(v0bd_made, 3)
            pe.wait_ge(wout0_in, 16 * 3)
            for y in range(3 * B):
                b, k = y // 3, y % 3
                if y >= 2:
                    pe.wait_ge(u_copied, y - 1)
                cs_in = [c for c, (h0, nh) in enumerate(HC) if h0 * KEY0 < (k + 1) * P and (h0 + nh) * KEY0 > k * P]
                mm_chain(ps[:, 6 + y % 2, 0:DM],
                         [(v0bd[0:HC[c][1] * D0, c, b, k * P:(k + 1) * P], wout0[0:HC[c][1] * D0, c, :]) for c in cs_in], u_mm)
            pe.wait_ge(q0_copied, 3 * B)
            pe.wait_ge(k0bd_made, 3)

            def evacuated(u):
                if u[0] == "v":
                    pe.wait_ge(v_copied, u[1] * NKT + u[2] + 1)
                else:
                    pe.wait_ge(rest_done, split_no[u] + 1)

            def project(u, f):
                bank = PROJ[f % 3]
                if f >= 3:
                    evacuated(order[f - 3])
                if u[0] == "k":
                    _, b, c, h = u
                    r0, n = CH[c]
                    if c < 2:
                        mm_chain(ps[:, bank, :], [(wk1[0:m, k, r0:r0 + n], cT[0:m, k, b * SK + h * 512:b * SK + h * 512 + 512])
                                                  for k, (_, m) in enumerate(CC)], proj_mm)
                    else:
                        for k, (_, m) in enumerate(CC):
                            for h in range(2):
                                mm = pe.matmul(ps[n * h:n * h + n, bank, :], wk1[0:m, k, r0:r0 + n],
                                               cT[0:m, k, b * SK + h * 512:b * SK + h * 512 + 512], start=(k == 0), stop=(k == 1))
                        mm.then_inc(proj_mm, 1)
                elif u[0] == "v":
                    _, b, t = u
                    mm_chain(ps[:, bank, 0:DM], [(cT[0:m, k, b * SK + t * P:b * SK + (t + 1) * P], wv1[0:m, k, :])
                                                 for k, (_, m) in enumerate(CC)], proj_mm)
                else:
                    _, b, c = u
                    r0, n = CH[c]
                    pe.wait_ge(x1T_copied, 2 * TB * (b + 1))
                    mm_chain(ps[0:n, bank, :], [(wq1[0:m, k, r0:r0 + n], xT[0:m, k, b * SQ:(b + 1) * SQ])
                                                for k, (_, m) in enumerate(CH)], proj_mm)

            f = 0
            for s in range(STEPS):
                if s < NT:
                    if s >= 2:
                        pe.wait_ge(sub0_done, s - 1)
                    for c, (h0, nh) in enumerate(HC):
                        n = nh * D0
                        m = pe.matmul(ps[:, s % 2, h0 * KEY0:(h0 + nh) * KEY0], q0T[0:n, c, s * P:(s + 1) * P],
                                      k0bd[0:n, c, s // TB, 0:nh * KEY0], start=True, stop=True)
                    m.then_inc(s0_mm, 1)
                if 2 <= s < NT + 2:
                    t = s - 2
                    pe.wait_ge(norm0_done, t + 1)
                    if t >= 1:
                        pe.wait_ge(pT_copied, t)
                    for k in range(3):
                        m = pe.transpose(ps[:, 2, k * P:(k + 1) * P], d0[:, t % 2, k * P:(k + 1) * P], ident_f[:, :])
                    m.then_inc(pT_mm, 1)
                if 3 <= s < NT + 3:
                    t = s - 3
                    pe.wait_ge(pT_copied, t + 1)
                    if t >= 1:
                        pe.wait_ge(x1_added, t)
                    mm_chain(ps[:, 3, 0:DM], [(pT[:, t % 2, k * P:(k + 1) * P], U[:, t // TB, k, :]) for k in range(3)], x1_mm)
                if 4 <= s < NT + 4:
                    t = s - 4
                    pe.wait_ge(x1_added, t + 1)
                    if t >= 1:
                        pe.wait_ge(x1T_copied, 2 * t)
                    for c, (r0, n) in enumerate(CH):
                        m = pe.transpose(ps[0:n, 4, c * P:(c + 1) * P], xs[:, t, r0:r0 + n], ident_f[:, :])
                    m.then_inc(x1T_mm, 1)
                if s == 0:
                    pe.wait_ge(wkv1_in, 16 * 4)
                    pe.wait_ge(u_copied, 3 * B)
                if s == NT:
                    pe.wait_ge(wq1_in, 16 * 3)
                for u in plan[s]:
                    project(u, f)
                    f += 1

            per_load = 16 * 2 * len(NPAIR)

            def max_scores(g, j, u):
                h, qt, half = u // (2 * TB), u // 2 % TB, u % 2
                n = g * UNITS + u
                if not isinstance(n, int) or n >= 2:
                    pe.wait_ge(max_done, n - 1)
                pe.matmul(ps[:, u % 2, :], QS[0:STK, j, h, qt * P:(qt + 1) * P], KS[0:STK, j, h, half * 512:half * 512 + 512],
                          start=True, stop=True).then_inc(max_mm, 1)

            def neg_rows(g):
                pe.wait_ge(neg_done, g + 1)
                for qt in range(TB):
                    m = pe.transpose(ps7b[0:3 * GH, qt * P:(qt + 1) * P], neg_p[:, :, :, qt], ident_b[:, :])
                m.then_inc(mT_mm, 1)

            def scores(g, j, kt, p, n=None):
                n = g * 16 + (2 * kt + p)
                if not isinstance(n, int) or n >= 2:
                    pe.wait_ge(exp_done, n - 1)
                for h in (2 * p, 2 * p + 1):
                    m = pe.matmul(ps[:, 2 + h, :], KS[0:STK + 3, j, h, kt * P:(kt + 1) * P], QS[0:STK + 3, j, h, :],
                                  start=True, stop=True)
                m.then_inc(s_mm, 1)

            def values(g, j, kt):
                pe.wait_ge(exp_done, g * 16 + (2 * kt + 2))
                for h in range(GH):
                    m = pe.matmul(ps[2 * D1 * h:2 * D1 * (h + 1), 6, :], VS[:, j, kt, h, :],
                                  probs[:, (2 * kt + h // 2) % 4, h % 2, :], start=(kt == 0), stop=(kt == NKT - 1))
                m.then_inc(pv_mm, 1)

            def turn_o(g):
                pe.wait_ge(o_copied, g)
                if not isinstance(g, int) or g < NG:
                    pe.wait_ge(mT_copied, g + 1)
                for qt in range(TB):
                    m = pe.transpose(ps[:, 7, qt * P:(qt + 1) * P], o_raw[:, qt * P:(qt + 1) * P], ident_f[:, :])
                m.then_inc(oT_mm, 1)

            def final_turn(t):
                b, qt = t // TB, t % TB
                if t < TB:
                    pe.wait_ge(o_norm, GB)
                    if t == 0:
                        pe.wait_ge(max_done, NG * UNITS)
                    else:
                        pe.wait_ge(fT_copied, 2 * t)
                else:
                    pe.wait_ge(o_norm, NG)
                    pe.wait_ge(fT_copied, 2 * (t - 1))
                bk = 0 if t < TB else 2 + t % 2
                for c in range(2):
                    pe.transpose(ps[:, bk, c * P:(c + 1) * P], attn[:, qt, b * GB + 2 * c:b * GB + 2 * c + 2, :].rearrange("p g n -> p (g n)"), ident_f[:, :])
                pe.transpose(ps[0:64, bk, 2 * P:3 * P], attn[:, qt, b * GB + 4, :], ident_f[:, :]).then_inc(fT_mm, 1)

            def final_mm(t):
                pe.wait_ge(fT_copied, 2 * t + 2)
                pe.wait_ge(wo1_in, 16 * 3)
                if t < TB:
                    if t >= 1:
                        pe.wait_ge(fin_added, t)
                else:
                    pe.wait_ge(fin_added, t - 1)
                bk = 1 if t < TB else 4 + t % 2
                mm_chain(ps[:, bk, 0:DM], [(oT[0:n, t % 2, c, :], wo1[0:n, c, :]) for c, (_, n) in enumerate(CH)], fin_mm)

            def group(g, j, i, last):
                for kt in range(NKT):
                    units = []
                    if not last:
                        lead = kt >= NKT - 2
                        units = list(range(PER * (kt - NKT + 2), PER * (kt - NKT + 3))) if lead else \
                            list(range(LEAD + PER * kt, LEAD + PER * kt + PER))
                    ahead = j + (2 if kt >= NKT - 2 else 1)
                    gg, jj = g + ahead - j, ahead % BUF
                    if kt < NKT - 1:
                        scores(g, j, kt + 1, 0)
                    if kt == 0 and not last:
                        pe.wait_ge(stack_in[jj], (i + ahead // BUF + 1) * per_load)
                    if units:
                        if kt < NKT - 2 or j < BUF - 1:
                            if kt == NKT - 2:
                                pe.wait_ge(stack_in[jj], (i + ahead // BUF + 1) * per_load)
                            for u in units[:2]:
                                max_scores(gg, jj, u)
                            if kt < NKT - 1:
                                scores(g, j, kt + 1, 1)
                            for u in units[2:]:
                                max_scores(gg, jj, u)
                        else:
                            if kt < NKT - 1:
                                scores(g, j, kt + 1, 1)
                            with pe.If(i < NG // BUF - 1):
                                if kt == NKT - 2:
                                    pe.wait_ge(stack_in[jj], (i + ahead // BUF + 1) * per_load)
                                for u in units:
                                    max_scores(gg, jj, u)
                    elif kt < NKT - 1:
                        scores(g, j, kt + 1, 1)
                    if kt == NKT - 1 and not last:
                        pe.wait_ge(m_in, g * 16 + 32)
                        scores(g + 1, (j + 1) % BUF, 0, 0)
                        scores(g + 1, (j + 1) % BUF, 0, 1)
                    if kt == 0:
                        if j > 0 or last:
                            turn_o(g)
                        else:
                            with pe.If(i > 0):
                                turn_o(g)
                        pe.wait_ge(v_staged, g + 1)
                    values(g, j, kt)
                    if kt == NKT - 2 and not last:
                        neg_rows(g + 1)
                    if last:
                        if kt % 2 == 0:
                            final_turn(kt // 2)
                        else:
                            final_mm(kt // 2)

            pe.wait_ge(id_ready, 2)
            pe.wait_ge(ones_ready, 3)
            pe.wait_ge(sub0_done, NT)
            pe.wait_ge(stack_in[0], per_load)
            for u in range(UNITS):
                max_scores(0, 0, u)
            pe.wait_ge(stack_in[1], per_load)
            for u in range(LEAD):
                max_scores(1, 1, u)
            for u in order[-3:]:
                evacuated(u)
            neg_rows(0)
            pe.wait_ge(x1T_copied, 2 * NT)
            pe.wait_ge(m_in, 16)
            scores(0, 0, 0, 0)
            scores(0, 0, 0, 1)
            with pe.Fori(0, NG // BUF) as i:
                for j in range(BUF):
                    group(i * BUF + j, j, i, False)
            group(NG - 1, 0, None, True)
            turn_o(NG)
            final_turn(TB)
            for t in range(TB, NT):
                if t + 1 < NT:
                    final_turn(t + 1)
                final_mm(t)


_INS = ['x', 'ctx_768', 'L0_xattn_w_q', 'L0_xattn_w_k', 'L0_xattn_w_v', 'L0_xattn_w_k_dis', 'L0_xattn_w_v_dis',
        'L0_xattn_w_out', 'L0_xattn_b_out', 'L1_xattn_Wq', 'L1_xattn_Wk', 'L1_xattn_Wv', 'L1_xattn_Wo', 'L1_xattn_bo']
_OUTS = [((2, 512, 320), 'float32')]


def kernel(**inputs):
    import numpy as _np
    import concourse.bacc as _bacc
    from concourse import mybir as _mybir
    from concourse.bass_utils import run_bass_kernel_spmd as _run

    nc = _bacc.Bacc("TRN2", target_bir_lowering=False, num_devices=1)
    arrays, args = {}, []
    for name in _INS:
        a = _np.ascontiguousarray(inputs[name])
        arrays[f"in_{name}_dram"] = a
        args.append(nc.dram_tensor(f"in_{name}_dram", a.shape, _mybir.dt.from_np(a.dtype), kind="ExternalInput").ap())
    for i, (shape, dtype) in enumerate(_OUTS):
        dt = _mybir.dt.from_np(_np.dtype(dtype))
        args.append(nc.dram_tensor(f"out_{i}_dram", shape, dt, kind="ExternalOutput").ap())
    two_layer_cross_attention(nc, *args)
    r = _run(nc, [arrays], core_ids=[0])
    got = tuple(r.results[0][f"out_{i}_dram"] for i in range(len(_OUTS)))
    return got[0]
```

```python
import concourse.bass as bass
import numpy as np
from concourse import mybir
from contextlib import ExitStack

ALU = mybir.AluOpType
ACT = mybir.ActivationFunctionType
AX = mybir.AxisListType
F32 = mybir.dt.float32
BF16 = mybir.dt.bfloat16


def two_layer_cross_attention(nc, x, ctx_768, w_q0, w_k0, w_v0, w_kd0, w_vd0, w_out0, b_out0,
                              w_q1, w_k1, w_v1, w_o1, b_o1, out):
    B, SQ, DM = x.shape
    SK, DC = ctx_768.shape[1:]
    P = 128
    NT = B * SQ // P
    TB = NT // B
    NKT = SK // P
    H0, D0, NS, TOK = 8, 40, 3, 16
    SETS = (0, SK - TOK, TOK)
    KEY0 = NS * TOK
    COL0 = H0 * KEY0
    H1, D1, GH = 20, 16, 4
    GW = GH * D1
    GB = H1 // GH
    NG = B * GB
    CH = [(0, 128), (128, 128), (256, 64)]
    CC = [(0, 128), (128, 64)]
    HC = [(0, 3), (3, 3), (6, 2)]
    NPAIR = [(0, 0), (0, 1), (0, 2), (1, 0), (1, 1), (2, 0)]
    STK = len(NPAIR) * D1
    PB = 3
    BUF = 3
    LEAD = 12
    UNITS = GH * TB * 2
    MAX_BANK = [[0, 1, 0], [1, 0, 7, 1], [0, 7, 1, 0, 7], [1, 0, 7, 1], [0, 7, 1, 0], [1, 0, 1], [0, 1, 7, 0, 1], [7, 0, 1, 7]]
    PLACE = [sum(len(m) for m in MAX_BANK[:kt]) for kt in range(NKT)]
    KT_LEAD = PLACE.index(UNITS - LEAD)
    BANK_AT = sum(MAX_BANK, [])
    assert len(BANK_AT) == UNITS
    FREED_BY = []
    for at in range(UNITS):
        FREED_BY.append(next(d for d in range(1, UNITS + 1) if BANK_AT[at - d] == BANK_AT[at]))
    TAIL_BANK = (0, 1, 3, 4)

    k_parts = nc.dram_tensor("k_parts", [3, B * DM, SK], BF16, kind="Internal").ap()
    q_parts = nc.dram_tensor("q_parts", [3, B * DM, SQ], BF16, kind="Internal").ap()

    with ExitStack() as ctx:
        def sb(name, shape, dt=F32):
            return ctx.enter_context(nc.sbuf_tensor(name, shape, dt))

        def sem(name):
            return ctx.enter_context(nc.semaphore(name))

        ident_f = sb("ident_f", [P, P])
        ident_b = sb("ident_b", [P, P], BF16)
        xs = sb("xs", [P, NT, DM])
        cs = sb("cs", [P, B * NKT, DC])
        attn = cs[:, :, :].rearrange("p t n -> p (t n)")[:, 0:NG * TB * GW].rearrange(
            "p (q g n) -> p q g n", g=NG, q=TB)
        xT = sb("xT", [P, 3, B * SQ])
        cT = sb("cT", [P, 2, B * SK])
        tokT = sb("tokT", [P, 2, B, NS, TOK])
        wq0 = sb("wq0", [P, 3, DM])
        wk0 = sb("wk0", [P, 2, DM])
        wv0 = sb("wv0", [P, 2, DM])
        wkd0 = sb("wkd0", [P, 2, DM])
        wvd0 = sb("wvd0", [P, 2, DM])
        wout0 = sb("wout0", [P, 3, DM])
        wq1 = sb("wq1", [P, 3, DM])
        wk1 = sb("wk1", [P, 2, DM])
        wv1 = sb("wv1", [P, 2, DM])
        wo1 = sb("wo1", [P, 3, DM])
        bias0 = sb("bias0", [P, DM])
        bias1 = sb("bias1", [P, DM])
        mask_k = sb("mask_k", [P, 3 * KEY0])
        mask_v = sb("mask_v", [P, 3 * KEY0])
        U = sb("U", [P, B, 3, DM])
        d0 = sb("d0", [P, 2, COL0])
        max0 = sb("max0", [P, 2, H0 * NS])
        sum0 = sb("sum0", [P, 2, H0 * NS])
        rec0 = sb("rec0", [P, 2, H0 * NS])
        parts = sb("parts", [P, PB, 3, 512], BF16)
        rest = sb("rest", [P, 2, 512])
        KS = sb("KS", [P, BUF, GH, SK], BF16)
        QS = sb("QS", [P, BUF, GH, SQ], BF16)
        q0T = QS[:, :, :, :].rearrange("p a b c -> p (a b c)").bitcast(F32).rearrange(
            "p (c t) -> p c t", c=3)
        V = sb("V", [P, NG, NKT, GW])
        VS = sb("VS", [P, BUF, NKT, GH, 2 * D1])
        probs = sb("probs", [P, 4, 2, SQ])
        pr = probs[:, :, :, :].rearrange("p a b c -> p (a b c)")
        nk, nv = 3 * B * 3 * KEY0, 3 * B * COL0
        k0bd = pr[:, 0:nk].rearrange("p (c b n) -> p c b n", c=3, b=B)
        v0bd = pr[:, nk:nk + nv].rearrange("p (c b n) -> p c b n", c=3, b=B)
        pT = pr[:, nk + nv:nk + nv + 2 * COL0].rearrange("p (r n) -> p r n", r=2)
        o_raw = sb("o_raw", [P, SQ])
        o_turned = sb("o_turned", [P, SQ])
        o_rec = sb("o_rec", [P, TB * GH])
        mx = sb("mx", [P, BUF, UNITS])
        neg = sb("neg", [P, TB * GH])
        neg_r = sb("neg_r", [P, TB * GH])
        one = sb("one", [P, TB * GH])
        neg_p = sb("neg_p", [P, 3, GH, TB], BF16)
        mT = sb("mT", [3 * GH, SQ], BF16)
        oT = sb("oT", [P, 2, 3, P])
        ps = ctx.enter_context(nc.psum_tensor("ps", [P, 8, 512], F32))

        x_in = [sem(f"x_in{b}") for b in range(B)]
        c_in = [sem(f"c_in{b}") for b in range(B)]
        wq0_in, wkv0_in, wout0_in = sem("wq0_in"), sem("wkv0_in"), sem("wout0_in")
        wq1_in, wk1_in, wv1_in, wo1_in, bias_in = sem("wq1_in"), sem("wk1_in"), sem("wv1_in"), sem("wo1_in"), sem("bias_in")
        id_step, id_ready, mask_step, mask_ready = sem("id_step"), sem("id_ready"), sem("mask_step"), sem("mask_ready")
        zero_ready, ones_ready = sem("zero_ready"), sem("ones_ready")
        xT_mm, xT_copied = sem("xT_mm"), sem("xT_copied")
        cT_mm, cT_copied = sem("cT_mm"), sem("cT_copied")
        q0_mm, q0_copied = sem("q0_mm"), sem("q0_copied")
        tok_copied = sem("tok_copied")
        kv0_mm, k0bd_made, v0bd_made = sem("kv0_mm"), sem("k0bd_made"), sem("v0bd_made")
        u_mm, u_copied = sem("u_mm"), sem("u_copied")
        s0_mm, max0_done, sub0_done = sem("s0_mm"), sem("max0_done"), sem("sub0_done")
        exp0_done, sum0_done, rec0_done, norm0_done = sem("exp0_done"), sem("sum0_done"), sem("rec0_done"), sem("norm0_done")
        pT_mm, pT_copied = sem("pT_mm"), sem("pT_copied")
        xb_done, x1_mm, x1_added = sem("xb_done"), sem("x1_mm"), sem("x1_added")
        x1T_mm, x1T_copied, x1b_done = sem("x1T_mm"), sem("x1T_copied"), sem("x1b_done")
        proj_mm, v_copied = sem("proj_mm"), sem("v_copied")
        hi_done, rest_done, mid_done, lo_done = sem("hi_done"), sem("rest_done"), sem("mid_done"), sem("lo_done")
        stored = [sem(f"stored{k}") for k in range(16)]
        stack_in = [sem(f"stack_in{j}") for j in range(BUF)]
        v_staged, max_mm, max_done = sem("v_staged"), sem("max_mm"), sem("max_done")
        neg_made, neg_step, neg_done, mT_mm, turned_read, m_in = sem("neg_made"), sem("neg_step"), sem("neg_done"), sem("mT_mm"), sem("turned_read"), sem("m_in")
        s_mm, exp_done, pv_mm = sem("s_mm"), sem("exp_done"), sem("pv_mm")
        o_copied, oT_mm, o_rec_done, o_norm = sem("o_copied"), sem("oT_mm"), sem("o_rec_done"), sem("o_norm")
        fT_mm, fT_copied, fin_mm, fin_added, out_done = sem("fT_mm"), sem("fT_copied"), sem("fin_mm"), sem("fin_added"), sem("out_done")

        k_units = [[("k", b, c, h) for c in (0, 1) for h in range(2)] + [("k", b, 2, 0)] for b in range(B)]
        v_units = [[("v", b, t) for t in range(NKT)] for b in range(B)]
        q_units = [[("q", b, c) for c in range(3)] for b in range(B)]
        STEPS = NT + 4
        k0, v0 = k_units[0], v_units[0]
        plan = [k0[0:1], k0[1:2], k0[2:3], k0[3:4], k0[4:5], [], [], [], q_units[0], v0[0:2], v0[2:5], v0[5:8]]
        assert len(plan) == STEPS
        late = k_units[1] + q_units[1] + v_units[1]
        ahead_units = [(0, u) for u in range(UNITS)] + [(1, u) for u in range(LEAD)]
        tail, done = [], 0
        for n, u in enumerate(late):
            count = 0 if n == 0 else {"k": 3, "q": 4, "v": 3 if n % 2 else 2}[u[0]]
            tail.append((u, ahead_units[done:done + count]))
            done += count
        assert done >= len(ahead_units)
        TURN = 2 + next(n for n, (_, units) in enumerate(tail) if (0, UNITS - 1) in units)
        assert TURN < len(tail)
        order = [u for step in plan for u in step] + late
        split_no = {u: k for k, u in enumerate(u for u in order if u[0] != "v")}
        PROJ = (5, 6, 7)

        def stores_of(u):
            return 2 if u[0] == "k" and u[2] == 2 else 1

        def split_rows(u):
            return CH[u[2]][1] if u[0] == "q" or u[2] < 2 else P

        block = ctx.enter_context(nc.Block())

        def group_index(g):
            return g if isinstance(g, int) else g.with_bounds(min_val=0, max_val=NG - 1)

        def xT_bank(u):
            return (u if u < 3 else u + 3) % 4

        def q0_bank(w):
            return (w + 3 if w < 3 else w + 6) % 4

        def outputs_over_sums(g, o):
            dst = attn[:, :, bass.ds(group_index(g), 1), :].rearrange("p q o (h d) -> p q (o h) d", d=D1)
            o = o.rearrange("p (m c) -> p m c", c=2 * D1)[:, :, 0:D1].rearrange("p (q h) d -> p q h d", q=TB)
            return dst, o, o_rec[:, :].rearrange("p (q h) -> p q h", q=TB).unsqueeze(3).to_broadcast([P, TB, GH, D1])

        def load_weight(eng, dst, w, rows, s):
            whole, rest = w.shape[0] // rows, w.shape[0] % rows
            eng.dma_start(dst[0:rows, 0:whole, :], w[0:whole * rows, :].rearrange("(c p) n -> p c n", p=rows)).then_inc(s, 16)
            eng.dma_start(dst[0:rest, whole, :], w[whole * rows:, :]).then_inc(s, 16)

        @block.sync
        def _(sp):
            xv = x.rearrange("b (t p) n -> b p t n", p=P)
            for b in range(B):
                sp.dma_start(xs[:, b * TB:(b + 1) * TB, :], xv[b]).then_inc(x_in[b], 16)
            load_weight(sp, wv0, w_v0, P, wkv0_in)
            load_weight(sp, wvd0, w_vd0, P, wkv0_in)
            load_weight(sp, wout0, w_out0, HC[0][1] * D0, wout0_in)
            for dst, b in ((bias0, b_out0), (bias1, b_o1)):
                sp.dma_start(dst[:, :], b.partition_broadcast(P)).then_inc(bias_in, 16)
            load_weight(sp, wq1, w_q1, P, wq1_in)
            load_weight(sp, wo1, w_o1, P, wo1_in)

            def store(u):
                k = split_no[u]
                sp.wait_ge(lo_done, k + 1)
                r = k % PB
                if u[0] == "q":
                    r0, n = CH[u[2]]
                    dst = q_parts[:, u[1] * DM + r0:u[1] * DM + r0 + n, :].rearrange("a r n -> r a n")
                    sp.dma_start(dst, parts[0:n, r, :, :]).then_inc(stored[k], 16)
                elif u[2] < 2:
                    r0, n = CH[u[2]]
                    dst = k_parts[:, u[1] * DM + r0:u[1] * DM + r0 + n, u[3] * 512:u[3] * 512 + 512].rearrange("a r n -> r a n")
                    sp.dma_start(dst, parts[0:n, r, :, :]).then_inc(stored[k], 16)
                else:
                    r0, n = CH[2]
                    for h in range(2):
                        dst = k_parts[:, u[1] * DM + r0:u[1] * DM + r0 + n, h * 512:h * 512 + 512].rearrange("a r n -> r a n")
                        sp.dma_start(dst, parts[n * h:n * h + n, r, :, :]).then_inc(stored[k], 16)

            def load(g, j):
                for n, (pq, pk) in enumerate(NPAIR):
                    kv = k_parts[pk, bass.ds(group_index(g) * GW, GW), :].rearrange("(h d) n -> d h n", d=D1)
                    qv = q_parts[pq, bass.ds(group_index(g) * GW, GW), :].rearrange("(h d) n -> d h n", d=D1)
                    sp.dma_start(KS[n * D1:n * D1 + D1, j, :, :], kv).then_inc(stack_in[j], 16)
                    sp.dma_start(QS[n * D1:n * D1 + D1, j, :, :], qv).then_inc(stack_in[j], 16)

            def scratch_written(b):
                for u in k_units[b] + q_units[b]:
                    sp.wait_ge(stored[split_no[u]], 16 * stores_of(u))

            for u in k_units[0] + q_units[0]:
                store(u)
            scratch_written(0)
            sp.wait_ge(s0_mm, NT)
            load(0, 0)
            for n, u in enumerate(k_units[1] + q_units[1]):
                if n == PB:
                    load(1, 1)
                store(u)
            scratch_written(1)

            def max_rows(g, j):
                sp.wait_ge(turned_read, 2 * g if not isinstance(g, int) or g else 1)
                sp.dma_start(QS[STK:STK + 3, j, :, :], mT[:, :]).then_inc(m_in, 16)

            max_rows(0, 0)
            with sp.Fori(0, NG // BUF) as i:
                for j in range(BUF):
                    g = i * BUF + j
                    if j < BUF - 1:
                        sp.wait_ge(s_mm, g * 16 + 1)
                        load(g + 2, (j + 2) % BUF)
                    else:
                        with sp.If(i < NG // BUF - 1):
                            sp.wait_ge(s_mm, g * 16 + 1)
                            load(g + 2, (j + 2) % BUF)
                    max_rows(g + 1, (j + 1) % BUF)
            for t in range(NT):
                sp.wait_ge(fin_added, t + 1)
                sp.dma_start(out.rearrange("b (t p) n -> (b t) p n", p=P)[t], xs[:, t, :]).then_inc(out_done, 16)
            sp.wait_ge(out_done, 16 * NT)

        @block.gpsimd
        def _(pool):
            def diagonal(m, done):
                pool.affine_select(out=m, in_=m, compare_op=ALU.not_equal, fill=1.0, base=0,
                                   pattern=[[-1, P]], channel_multiplier=1).then_inc(done, 1)

            pool.memset(ident_f[:, :], 0.0).then_inc(id_step, 1)
            pool.memset(ident_b[:, :], 0.0).then_inc(id_step, 1)
            pool.memset(mask_k[:, :], 1.0).then_inc(mask_step, 1)
            pool.wait_ge(id_step, 2)
            diagonal(ident_f[:, :], id_ready)
            diagonal(ident_b[:, :], id_ready)
            mk = mask_k[:, :].rearrange("p (h k) -> p h k", h=3)
            mv = mask_v[:, :].rearrange("p (h k) -> p h k", h=3)
            pool.wait_ge(mask_step, 1)
            pool.affine_select(out=mk, in_=mk, compare_op=ALU.is_ge, fill=0.0, base=0,
                               pattern=[[-D0, 3], [0, KEY0]], channel_multiplier=1).then_inc(mask_step, 1)
            pool.wait_ge(mask_step, 2)
            pool.affine_select(out=mk, in_=mk, compare_op=ALU.is_ge, fill=0.0, base=D0 - 1,
                               pattern=[[D0, 3], [0, KEY0]], channel_multiplier=-1).then_inc(mask_step, 1)
            pool.wait_ge(mask_step, 3)
            pool.tensor_scalar(mask_v[:, :], mask_k[:, :], 0.5, None, ALU.mult).then_inc(mask_step, 1)
            pool.wait_ge(mask_step, 4)
            pool.tensor_scalar(mv[:, :, TOK:2 * TOK], mk[:, :, TOK:2 * TOK], 1.0, None, ALU.mult).then_inc(mask_ready, 1)
            pool.memset(v0bd, 0.0).then_inc(zero_ready, 1)
            pair_of_ones = float(np.array([0x3F803F80], np.uint32).view(np.float32)[0])
            pool.wait_ge(mask_ready, 1)
            pool.wait_ge(zero_ready, 1)
            pool.memset(KS[STK:STK + 3, :, :, :].rearrange("p a b c -> p (a b c)").bitcast(F32), pair_of_ones).then_inc(ones_ready, 1)
            pool.wait_ge(ones_ready, 1)
            pool.memset(VS[:, :, :, :, :], 1.0).then_inc(ones_ready, 1)
            pool.memset(one[:, :], 1.0).then_inc(ones_ready, 1)
            for b in range(B):
                pool.wait_ge(x_in[b], 16)
                pool.wait_ge(xT_mm, 3 * b + 3)
                pool.wait_ge(bias_in, 32)
                xb = xs[:, b * TB:(b + 1) * TB, :]
                pool.tensor_tensor(xb, xb, bias0[:, :].unsqueeze(1).to_broadcast([P, TB, DM]), ALU.add).then_inc(xb_done, 1)
            def split(u):
                if u[0] == "v":
                    return
                k = split_no[u]
                n = split_rows(u)
                pool.wait_ge(mid_done, k + 1)
                pool.tensor_tensor(parts[0:n, k % PB, 2, :], rest[0:n, k % 2, :], parts[0:n, k % PB, 1, :],
                                   ALU.subtract).then_inc(lo_done, 1)

            for s in range(STEPS):
                if 1 <= s <= NT:
                    t = s - 1
                    pool.wait_ge(rec0_done, t + 1)
                    e = d0[:, t % 2, :].rearrange("p (g k) -> p g k", k=TOK)
                    rb = rec0[:, t % 2, :].unsqueeze(2).to_broadcast([P, H0 * NS, TOK])
                    pool.tensor_tensor(e, e, rb, ALU.mult).then_inc(norm0_done, 1)
                if 4 <= s < NT + 4:
                    t = s - 4
                    pool.wait_ge(x1T_mm, t + 1)
                    pool.tensor_tensor(xs[:, t, :], xs[:, t, :], bias1[:, :], ALU.add).then_inc(x1b_done, 1)
                for u in plan[s]:
                    split(u)

            def stage_v(g, j):
                src = V[:, bass.ds(group_index(g), 1), :, :].rearrange("p o k (h d) -> p (o k) h d", h=GH)
                pool.wait_ge(v_copied, B * NKT)
                pool.tensor_copy(VS[:, j, :, :, 0:D1], src).then_inc(v_staged, 1)

            def neg_parts(g):
                pool.wait_ge(neg_made, g + 1)
                pool.wait_ge(mT_mm, g)
                pv = [neg_p[:, a, :, :].rearrange("p h q -> p (h q)") for a in range(3)]
                pool.tensor_tensor(pv[0], neg[:, :], one[:, :], ALU.mult).then_inc(neg_step, 1)
                pool.wait_ge(neg_step, g * 3 + 1)
                pool.tensor_tensor(neg_r[:, :], neg[:, :], pv[0], ALU.subtract).then_inc(neg_step, 1)
                pool.wait_ge(neg_step, g * 3 + 2)
                pool.tensor_tensor(pv[1], neg_r[:, :], one[:, :], ALU.mult).then_inc(neg_step, 1)
                pool.wait_ge(neg_step, g * 3 + 3)
                pool.tensor_tensor(pv[2], neg_r[:, :], pv[1], ALU.subtract).then_inc(neg_done, 1)

            def divide(g):
                pool.wait_ge(o_rec_done, g + 1)
                pool.tensor_tensor(*outputs_over_sums(g, o_turned[:, :]), ALU.mult).then_inc(o_norm, 1)

            pool.wait_ge(ones_ready, 3)
            for u, _ in tail:
                split(u)
            neg_parts(0)
            stage_v(0, 0)
            with pool.Fori(0, NG // BUF) as i:
                for j in range(BUF):
                    g = i * BUF + j
                    pool.wait_ge(s_mm, g * 16 + 1)
                    stage_v(g + 1, (j + 1) % BUF)
                    if j > 0:
                        divide(g - 1)
                    else:
                        with pool.If(i > 0):
                            divide(g - 1)
                    neg_parts(g + 1)
            divide(NG - 2)

        @block.scalar
        def _(act):
            load_weight(act, wq0, w_q0, P, wq0_in)
            cv = ctx_768.rearrange("b (t p) n -> b p t n", p=P)
            for b in range(B):
                act.dma_start(cs[:, b * NKT:(b + 1) * NKT, :], cv[b]).then_inc(c_in[b], 16)
            load_weight(act, wk0, w_k0, P, wkv0_in)
            load_weight(act, wkd0, w_kd0, P, wkv0_in)
            load_weight(act, wk1, w_k1, P, wk1_in)
            load_weight(act, wv1, w_v1, P, wv1_in)
            def copy_q0(b):
                for c in range(3):
                    w = 3 * b + c
                    n = HC[c][1] * D0
                    act.wait_ge(q0_mm, w + 1)
                    act.copy(q0T[0:n, c, b * SQ:(b + 1) * SQ], ps[0:n, q0_bank(w), :]).then_inc(q0_copied, 1)

            copy_q0(0)
            for v in range(8):
                qd, c = v // 2, v % 2
                n = CC[c][1]
                act.wait_ge(cT_mm, v + 1)
                act.copy(cT[0:n, c, qd * 512:qd * 512 + 512], ps[0:n, 4 + v % 4, :]).then_inc(cT_copied, 1)
            copy_q0(1)
            for y in range(3 * B):
                b, k = y // 3, y % 3
                act.wait_ge(u_mm, y + 1)
                act.copy(U[:, b, k, :], ps[:, 6 + y % 2, 0:DM]).then_inc(u_copied, 1)

            behind = []

            def second_part():
                while behind:
                    k, n = behind.pop()
                    act.wait_ge(rest_done, k + 1)
                    act.copy(parts[0:n, k % PB, 1, :], rest[0:n, k % 2, :]).then_inc(mid_done, 1)

            def take(u, f):
                second_part()
                act.wait_ge(proj_mm, f + 1)
                if u[0] == "v":
                    g0 = u[1] * GB
                    act.copy(V[:, g0:g0 + GB, u[2], :], ps[:, PROJ[f % 3], 0:DM].rearrange("p (g n) -> p g n", g=GB)).then_inc(v_copied, 1)
                    return
                k = split_no[u]
                n = split_rows(u)
                if k >= PB:
                    old = [w for w in split_no if split_no[w] == k - PB][0]
                    act.wait_ge(stored[k - PB], 16 * stores_of(old))
                act.copy(parts[0:n, k % PB, 0, :], ps[0:n, PROJ[f % 3], :]).then_inc(hi_done, 1)
                behind.append((k, n))

            def mT_copy(g, bank=7):
                act.wait_ge(mT_mm, g + 1)
                if not isinstance(g, int):
                    act.wait_ge(m_in, g * 16)
                act.copy(mT[:, :], ps[:, bank, :].bitcast(BF16)[0:3 * GH, 0:SQ]).then_inc(turned_read, 1)

            f = 0
            for s in range(STEPS):
                if s < NT:
                    act.wait_ge(sub0_done, s + 1)
                    act.activation(d0[:, s % 2, :], d0[:, s % 2, :], ACT.Exp, scale=float(D0) ** -0.5).then_inc(exp0_done, 1)
                second_part()
                if 2 <= s < NT + 2:
                    t = s - 2
                    act.wait_ge(pT_mm, t + 1)
                    if t >= 2:
                        act.wait_ge(x1_mm, t - 1)
                    act.copy(pT[:, t % 2, :], ps[:, 2, 0:COL0]).then_inc(pT_copied, 1)
                if 4 <= s < NT + 4:
                    t = s - 4
                    act.wait_ge(x1T_mm, t + 1)
                    act.copy(xT[:, 0:2, t * P:(t + 1) * P], ps[:, 4, 0:2 * P].rearrange("p (c n) -> p c n", c=2)).then_inc(x1T_copied, 1)
                    act.copy(xT[0:64, 2, t * P:(t + 1) * P], ps[0:64, 4, 2 * P:3 * P]).then_inc(x1T_copied, 1)
                for u in plan[s]:
                    take(u, f)
                    f += 1
            for n, (u, _) in enumerate(tail):
                take(u, f)
                f += 1
                if n == TURN:
                    mT_copy(0, 2)

            def exp_pair(g, kt, p):
                n = g * 16 + (2 * kt + p)
                act.wait_ge(s_mm, n + 1)
                if kt >= 2:
                    act.wait_ge(pv_mm, g * NKT + (kt - 1))
                act.activation(probs[:, (2 * kt + p) % 4, :, :], ps[:, 2 + 2 * p:4 + 2 * p, :], ACT.Exp,
                               scale=float(D1) ** -0.5).then_inc(exp_done, 1)

            def copy_o(g):
                act.wait_ge(pv_mm, g * NKT + NKT)
                act.copy(o_raw[:, :], ps[:, 6, :]).then_inc(o_copied, 1)

            def copy_turned(g):
                act.wait_ge(oT_mm, g + 1)
                act.copy(o_turned[:, :], ps[:, 7, :]).then_inc(turned_read, 1)

            def copy_final(t):
                act.wait_ge(fT_mm, t + 1)
                if t >= 2:
                    act.wait_ge(fin_mm, t - 1)
                bk = 0 if t < TB else 2 + t % 2
                act.copy(oT[:, t % 2, 0:2, :], ps[:, bk, 0:2 * P].rearrange("p (c n) -> p c n", c=2)).then_inc(fT_copied, 1)
                act.copy(oT[0:64, t % 2, 2, :], ps[0:64, bk, 2 * P:3 * P]).then_inc(fT_copied, 1)

            def group(g, j, i, last):
                for kt in range(NKT):
                    if kt == 0:
                        if j > 0 or last:
                            copy_o(g - 1)
                        else:
                            with act.If(i > 0):
                                copy_o(g - 1)
                    if kt < NKT - 1:
                        exp_pair(g, kt + 1, 0)
                        exp_pair(g, kt + 1, 1)
                        if kt == 0:
                            if j > 0 or last:
                                copy_turned(g - 1)
                            else:
                                with act.If(i > 0):
                                    copy_turned(g - 1)
                    elif not last:
                        for p in range(2):
                            n = g * 16 + 16 + p
                            act.wait_ge(s_mm, n + 1)
                            act.wait_ge(pv_mm, g * NKT + (NKT - 1))
                            act.activation(probs[:, p, :, :], ps[:, 2 + 2 * p:4 + 2 * p, :], ACT.Exp,
                                           scale=float(D1) ** -0.5).then_inc(exp_done, 1)
                    if kt == KT_LEAD and not last:
                        mT_copy(g + 1)
                    if last and kt % 2 == 0:
                        copy_final(kt // 2)

            exp_pair(0, 0, 0)
            exp_pair(0, 0, 1)
            with act.Fori(0, NG // BUF) as i:
                for j in range(BUF):
                    group(i * BUF + j, j, i, False)
            group(NG - 1, 0, None, True)
            copy_o(NG - 1)
            for t in range(TB, NT):
                copy_final(t)

        @block.vector
        def _(dve):
            for u in range(3 * B):
                b, c = u // 3, u % 3
                n = CH[c][1]
                dve.wait_ge(xT_mm, u + 1)
                dve.tensor_copy(xT[0:n, c, b * SQ:(b + 1) * SQ], ps[0:n, xT_bank(u), :]).then_inc(xT_copied, 1)
            dve.wait_ge(cT_copied, 8)
            for k, (_, n) in enumerate(CC):
                for st, t0 in enumerate(SETS):
                    dve.tensor_copy(tokT[0:n, k, :, st, :], cT[0:n, k, :].rearrange("p (b n) -> p b n", b=B)[:, :, t0:t0 + TOK]).then_inc(tok_copied, 1)
            dve.wait_ge(mask_ready, 1)
            for kv, (bank, made, mask) in enumerate(((4, k0bd_made, mask_k), (5, v0bd_made, mask_v))):
                dve.wait_ge(kv0_mm, kv + 1)
                if kv:
                    dve.wait_ge(zero_ready, 1)
                for c, (h0, nh) in enumerate(HC):
                    n = nh * D0
                    src = ps[0:n, bank, c * B * KEY0:(c + 1) * B * KEY0].rearrange("p (b k) -> p b k", b=B)
                    dst = v0bd[0:n, c, :, h0 * KEY0:(h0 + nh) * KEY0] if kv else k0bd[0:n, c, :, 0:nh * KEY0]
                    dve.tensor_tensor(dst.rearrange("p b (h k) -> p b h k", h=nh),
                                      src.unsqueeze(2).to_broadcast([n, B, nh, KEY0]),
                                      mask[0:n, 0:nh * KEY0].rearrange("p (h k) -> p h k", h=nh).unsqueeze(1).to_broadcast([n, B, nh, KEY0]),
                                      ALU.mult).then_inc(made, 1)

            def leave_rest(u, f):
                if u[0] == "v":
                    return
                k = split_no[u]
                n = split_rows(u)
                dve.wait_ge(hi_done, k + 1)
                if k >= 2:
                    dve.wait_ge(lo_done, k - 1)
                dve.tensor_tensor(rest[0:n, k % 2, :], ps[0:n, PROJ[f % 3], :], parts[0:n, k % PB, 0, :],
                                  ALU.subtract).then_inc(rest_done, 1)

            def maximum(g, j, u, bank):
                n = g * UNITS + u
                dve.wait_ge(max_mm, n + 1)
                dve.tensor_reduce(mx[:, j, u:u + 1], ps[:, bank, :], AX.X, ALU.max).then_inc(max_done, 1)

            def negate(g, j):
                dve.wait_ge(max_done, g * UNITS + UNITS)
                dve.wait_ge(neg_done, g)
                dve.tensor_reduce(neg[:, :], mx[:, j, :].rearrange("p (m h) -> p m h", h=2), AX.X, ALU.max,
                                  negate=True).then_inc(neg_made, 1)

            f = 0
            for s in range(STEPS):
                if s < NT:
                    sc = ps[:, s % 2, 0:COL0].rearrange("p (g k) -> p g k", k=TOK)
                    dve.wait_ge(s0_mm, s + 1)
                    dve.tensor_reduce(max0[:, s % 2, :], sc, AX.X, ALU.max).then_inc(max0_done, 1)
                    dve.wait_ge(max0_done, s + 1)
                    if s >= 2:
                        dve.wait_ge(pT_mm, s - 1)
                    dve.tensor_tensor(d0[:, s % 2, :].rearrange("p (g k) -> p g k", k=TOK), sc,
                                      max0[:, s % 2, :].unsqueeze(2).to_broadcast([P, H0 * NS, TOK]),
                                      ALU.subtract).then_inc(sub0_done, 1)
                if 1 <= s <= NT:
                    t = s - 1
                    dve.wait_ge(exp0_done, t + 1)
                    dve.tensor_reduce(sum0[:, t % 2, :], d0[:, t % 2, :].rearrange("p (g k) -> p g k", k=TOK),
                                      AX.X, ALU.add).then_inc(sum0_done, 1)
                    dve.wait_ge(sum0_done, t + 1)
                    if t >= 2:
                        dve.wait_ge(norm0_done, t - 1)
                    dve.reciprocal(rec0[:, t % 2, :], sum0[:, t % 2, :]).then_inc(rec0_done, 1)
                if 3 <= s < NT + 3:
                    t = s - 3
                    dve.wait_ge(x1_mm, t + 1)
                    dve.wait_ge(xb_done, t // TB + 1)
                    dve.tensor_tensor(xs[:, t, :], ps[:, 3, 0:DM], xs[:, t, :], ALU.add).then_inc(x1_added, 1)
                for u in plan[s]:
                    leave_rest(u, f)
                    f += 1

            def invert_sums(g, o, read):
                dve.wait_ge(*read)
                dve.reciprocal(o_rec[:, :], o.rearrange("p (m c) -> p m c", c=2 * D1)[:, :, D1]).then_inc(o_rec_done, 1)

            def group(g, j, i, last):
                for kt in range(NKT):
                    if kt == 1:
                        if j > 0 or last:
                            invert_sums(g - 1, o_turned[:, :], (turned_read, 2 * g + 1))
                        else:
                            with dve.If(i > 0):
                                invert_sums(g - 1, o_turned[:, :], (turned_read, 2 * g + 1))
                    if last:
                        continue
                    ahead = j + (2 if kt >= KT_LEAD else 1)

                    def maxima():
                        for n, bank in enumerate(MAX_BANK[kt]):
                            maximum(g + ahead - j, ahead % BUF, (PLACE[kt] + n + LEAD) % UNITS, bank)

                    if kt < KT_LEAD or j < BUF - 1:
                        maxima()
                    else:
                        with dve.If(i < NG // BUF - 1):
                            maxima()
                    if kt == KT_LEAD - 1:
                        negate(g + 1, (j + 1) % BUF)

            for u, units in tail:
                leave_rest(u, f)
                f += 1
                for g, m in units:
                    maximum(g, g, m, TAIL_BANK[(g * UNITS + m) % len(TAIL_BANK)])
                    if (g, m) == (0, UNITS - 1):
                        negate(0, 0)
            with dve.Fori(0, NG // BUF) as i:
                for j in range(BUF):
                    group(i * BUF + j, j, i, False)

            def final(t):
                dve.wait_ge(fin_mm, t + 1)
                dve.wait_ge(x1b_done, t + 1)
                bk = 1 if t < TB else 4 + t % 2
                dve.tensor_tensor(xs[:, t, :], ps[:, bk, 0:DM], xs[:, t, :], ALU.add).then_inc(fin_added, 1)

            group(NG - 1, 0, None, True)
            for t in range(TB):
                final(t)
            g, o = NG - 1, ps[:, 7, :]
            dve.wait_ge(o_norm, g)
            invert_sums(g, o, (oT_mm, NG))
            dve.wait_ge(o_rec_done, NG)
            dve.tensor_tensor(*outputs_over_sums(g, o), ALU.mult).then_inc(o_norm, 1)
            for t in range(TB, NT):
                final(t)

        @block.tensor
        def _(pe):
            def mm_chain(dst, pairs, s=None):
                for n, (l, r) in enumerate(pairs):
                    m = pe.matmul(dst, l, r, start=(n == 0), stop=(n == len(pairs) - 1))
                if s is not None:
                    m.then_inc(s, 1)
                return m

            pe.wait_ge(id_ready, 1)
            def turn_x(b):
                pe.wait_ge(x_in[b], 16)
                for c, (r0, n) in enumerate(CH):
                    u = 3 * b + c
                    if b and c:
                        pe.wait_ge(q0_copied, c)
                    for k in range(TB):
                        m = pe.transpose(ps[0:n, xT_bank(u), k * P:(k + 1) * P], xs[:, b * TB + k, r0:r0 + n], ident_f[:, :])
                    m.then_inc(xT_mm, 1)

            def queries0(b):
                pe.wait_ge(wq0_in, 32)
                pe.wait_ge(xT_copied, 3 * b + 3)
                if b:
                    pe.wait_ge(q0_copied, 3)
                for c, (h0, nh) in enumerate(HC):
                    mm_chain(ps[0:nh * D0, q0_bank(3 * b + c), :],
                             [(wq0[0:n, k, h0 * D0:(h0 + nh) * D0], xT[0:n, k, b * SQ:(b + 1) * SQ]) for k, (_, n) in enumerate(CH)], q0_mm)

            turn_x(0)
            queries0(0)
            turn_x(1)
            for v in range(8):
                qd, c = v // 2, v % 2
                r0, n = CC[c]
                pe.wait_ge(c_in[qd // 2], 16)
                if v >= 4:
                    pe.wait_ge(cT_copied, v - 3)
                for k in range(4):
                    m = pe.transpose(ps[0:n, 4 + v % 4, k * P:(k + 1) * P], cs[:, qd * 4 + k, r0:r0 + n], ident_f[:, :])
                m.then_inc(cT_mm, 1)
            queries0(1)
            pe.wait_ge(tok_copied, 6)
            pe.wait_ge(wkv0_in, 16 * 8)
            for kv, (dis, anat) in enumerate(((wkd0, wk0), (wvd0, wv0))):
                for c, (h0, nh) in enumerate(HC):
                    dst = ps[0:nh * D0, 4 + kv, c * B * KEY0:(c + 1) * B * KEY0].rearrange("p (b s k) -> p b s k", b=B, s=NS)
                    for w, s0, s1 in ((dis, 0, 2), (anat, 2, 3)):
                        m = mm_chain(dst[:, :, s0:s1, :],
                                     [(w[0:n, k, h0 * D0:(h0 + nh) * D0], tokT[0:n, k, :, s0:s1, :]) for k, (_, n) in enumerate(CC)])
                m.then_inc(kv0_mm, 1)
            pe.wait_ge(v0bd_made, 3)
            pe.wait_ge(wout0_in, 32)
            for y in range(3 * B):
                b, k = y // 3, y % 3
                if y >= 2:
                    pe.wait_ge(u_copied, y - 1)
                cs_in = [c for c, (h0, nh) in enumerate(HC) if h0 * KEY0 < (k + 1) * P and (h0 + nh) * KEY0 > k * P]
                mm_chain(ps[:, 6 + y % 2, 0:DM],
                         [(v0bd[0:HC[c][1] * D0, c, b, k * P:(k + 1) * P], wout0[0:HC[c][1] * D0, c, :]) for c in cs_in], u_mm)
            pe.wait_ge(q0_copied, 3 * B)
            pe.wait_ge(k0bd_made, 3)

            def evacuated(u):
                if u[0] == "v":
                    pe.wait_ge(v_copied, u[1] * NKT + u[2] + 1)
                else:
                    pe.wait_ge(rest_done, split_no[u] + 1)

            def project(u, f):
                bank = PROJ[f % 3]
                if f >= 3:
                    evacuated(order[f - 3])
                if u[0] == "k":
                    _, b, c, h = u
                    r0, n = CH[c]
                    if c < 2:
                        mm_chain(ps[:, bank, :], [(wk1[0:m, k, r0:r0 + n], cT[0:m, k, b * SK + h * 512:b * SK + h * 512 + 512])
                                                  for k, (_, m) in enumerate(CC)], proj_mm)
                    else:
                        for k, (_, m) in enumerate(CC):
                            for h in range(2):
                                mm = pe.matmul(ps[n * h:n * h + n, bank, :], wk1[0:m, k, r0:r0 + n],
                                               cT[0:m, k, b * SK + h * 512:b * SK + h * 512 + 512], start=(k == 0), stop=(k == 1))
                        mm.then_inc(proj_mm, 1)
                elif u[0] == "v":
                    _, b, t = u
                    mm_chain(ps[:, bank, 0:DM], [(cT[0:m, k, b * SK + t * P:b * SK + (t + 1) * P], wv1[0:m, k, :])
                                                 for k, (_, m) in enumerate(CC)], proj_mm)
                else:
                    _, b, c = u
                    r0, n = CH[c]
                    pe.wait_ge(x1T_copied, 2 * TB * (b + 1))
                    mm_chain(ps[0:n, bank, :], [(wq1[0:m, k, r0:r0 + n], xT[0:m, k, b * SQ:(b + 1) * SQ])
                                                for k, (_, m) in enumerate(CH)], proj_mm)

            f = 0
            for s in range(STEPS):
                if s < NT:
                    if s >= 2:
                        pe.wait_ge(sub0_done, s - 1)
                    for c, (h0, nh) in enumerate(HC):
                        n = nh * D0
                        m = pe.matmul(ps[:, s % 2, h0 * KEY0:(h0 + nh) * KEY0], q0T[0:n, c, s * P:(s + 1) * P],
                                      k0bd[0:n, c, s // TB, 0:nh * KEY0], start=True, stop=True)
                    m.then_inc(s0_mm, 1)
                if 2 <= s < NT + 2:
                    t = s - 2
                    pe.wait_ge(norm0_done, t + 1)
                    if t >= 1:
                        pe.wait_ge(pT_copied, t)
                    for k in range(3):
                        m = pe.transpose(ps[:, 2, k * P:(k + 1) * P], d0[:, t % 2, k * P:(k + 1) * P], ident_f[:, :])
                    m.then_inc(pT_mm, 1)
                if 3 <= s < NT + 3:
                    t = s - 3
                    pe.wait_ge(pT_copied, t + 1)
                    if t >= 1:
                        pe.wait_ge(x1_added, t)
                    mm_chain(ps[:, 3, 0:DM], [(pT[:, t % 2, k * P:(k + 1) * P], U[:, t // TB, k, :]) for k in range(3)], x1_mm)
                if 4 <= s < NT + 4:
                    t = s - 4
                    pe.wait_ge(x1_added, t + 1)
                    if t >= 1:
                        pe.wait_ge(x1T_copied, 2 * t)
                    for c, (r0, n) in enumerate(CH):
                        m = pe.transpose(ps[0:n, 4, c * P:(c + 1) * P], xs[:, t, r0:r0 + n], ident_f[:, :])
                    m.then_inc(x1T_mm, 1)
                if s == 0:
                    pe.wait_ge(wk1_in, 32)
                    pe.wait_ge(u_copied, 3 * B)
                if s == NT:
                    pe.wait_ge(wq1_in, 32)
                    pe.wait_ge(wv1_in, 32)
                for u in plan[s]:
                    project(u, f)
                    f += 1

            per_load = 16 * 2 * len(NPAIR)

            def max_scores(j, u, bank):
                h, qt, half = u // (2 * TB), u // 2 % TB, u % 2
                pe.matmul(ps[:, bank, :], QS[0:STK, j, h, qt * P:(qt + 1) * P], KS[0:STK, j, h, half * 512:half * 512 + 512],
                          start=True, stop=True).then_inc(max_mm, 1)

            def neg_rows(g, bank=7):
                pe.wait_ge(neg_done, g + 1)
                for qt in range(TB):
                    m = pe.transpose(ps[:, bank, :].bitcast(BF16)[0:3 * GH, qt * P:(qt + 1) * P], neg_p[:, :, :, qt], ident_b[:, :])
                m.then_inc(mT_mm, 1)

            def scores(g, j, kt, p, n=None):
                n = g * 16 + (2 * kt + p)
                if not isinstance(n, int) or n >= 2:
                    pe.wait_ge(exp_done, n - 1)
                for h in (2 * p, 2 * p + 1):
                    m = pe.matmul(ps[:, 2 + h, :], KS[0:STK + 3, j, h, kt * P:(kt + 1) * P], QS[0:STK + 3, j, h, :],
                                  start=True, stop=True)
                m.then_inc(s_mm, 1)

            def values(g, j, kt):
                pe.wait_ge(exp_done, g * 16 + (2 * kt + 2))
                for h in range(GH):
                    m = pe.matmul(ps[2 * D1 * h:2 * D1 * (h + 1), 6, :], VS[:, j, kt, h, :],
                                  probs[:, (2 * kt + h // 2) % 4, h % 2, :], start=(kt == 0), stop=(kt == NKT - 1))
                m.then_inc(pv_mm, 1)

            def turn_o(g):
                pe.wait_ge(o_copied, g)
                if isinstance(g, int) and g == NG:
                    pe.wait_ge(turned_read, 2 * g - 1)
                elif isinstance(g, int):
                    pe.wait_ge(turned_read, 2 * g)
                else:
                    pe.wait_ge(turned_read, 2 * g)
                    pe.wait_ge(max_done, g * UNITS + UNITS + LEAD)
                for qt in range(TB):
                    m = pe.transpose(ps[:, 7, qt * P:(qt + 1) * P], o_raw[:, qt * P:(qt + 1) * P], ident_f[:, :])
                m.then_inc(oT_mm, 1)

            def final_turn(t):
                b, qt = t // TB, t % TB
                if t < TB:
                    pe.wait_ge(o_norm, GB)
                    if t == 0:
                        pe.wait_ge(max_done, NG * UNITS)
                    else:
                        pe.wait_ge(fT_copied, 2 * t)
                else:
                    pe.wait_ge(o_norm, NG)
                    pe.wait_ge(fT_copied, 2 * (t - 1))
                bk = 0 if t < TB else 2 + t % 2
                for c in range(2):
                    pe.transpose(ps[:, bk, c * P:(c + 1) * P], attn[:, qt, b * GB + 2 * c:b * GB + 2 * c + 2, :].rearrange("p g n -> p (g n)"), ident_f[:, :])
                pe.transpose(ps[0:64, bk, 2 * P:3 * P], attn[:, qt, b * GB + 4, :], ident_f[:, :]).then_inc(fT_mm, 1)

            def final_mm(t):
                pe.wait_ge(fT_copied, 2 * t + 2)
                pe.wait_ge(wo1_in, 32)
                if t < TB:
                    if t >= 1:
                        pe.wait_ge(fin_added, t)
                else:
                    pe.wait_ge(fin_added, t - 1)
                bk = 1 if t < TB else 4 + t % 2
                mm_chain(ps[:, bk, 0:DM], [(oT[0:n, t % 2, c, :], wo1[0:n, c, :]) for c, (_, n) in enumerate(CH)], fin_mm)

            def group(g, j, i, last):
                for kt in range(NKT):
                    ahead = j + (2 if kt >= KT_LEAD else 1)
                    gg, jj = g + ahead - j, ahead % BUF

                    def maxima(n0, n1):
                        if last or n0 == n1:
                            return
                        if n0 == 0 and kt in (0, KT_LEAD):
                            pe.wait_ge(stack_in[jj], (i + ahead // BUF + 1) * per_load)
                        for at in range(PLACE[kt] + n0, PLACE[kt] + n1):
                            u = (at + LEAD) % UNITS
                            pe.wait_ge(max_done, gg * UNITS + u + 1 - FREED_BY[at])
                            if at == BANK_AT.index(7):
                                pe.wait_ge(turned_read, 2 * g + 1)
                            if BANK_AT[at] == 7 and kt == KT_LEAD + 1:
                                pe.wait_ge(turned_read, 2 * g + 2)
                            max_scores(jj, u, BANK_AT[at])

                    def maxima_if(n0, n1):
                        if last or n0 == n1 or kt < KT_LEAD or j < BUF - 1:
                            maxima(n0, n1)
                        else:
                            with pe.If(i < NG // BUF - 1):
                                maxima(n0, n1)

                    maxima_if(0, 2)
                    if kt < NKT - 1:
                        scores(g, j, kt + 1, 0)
                    elif not last:
                        pe.wait_ge(m_in, g * 16 + 32)
                        scores(g + 1, (j + 1) % BUF, 0, 0)
                    count = len(MAX_BANK[kt])
                    late_from = min(3, count - 1)
                    maxima_if(2, late_from)
                    if kt < NKT - 1:
                        scores(g, j, kt + 1, 1)
                    elif not last:
                        scores(g + 1, (j + 1) % BUF, 0, 1)
                    if kt == 0:
                        if j > 0 or last:
                            turn_o(g)
                        else:
                            with pe.If(i > 0):
                                turn_o(g)
                        pe.wait_ge(v_staged, g + 1)
                    maxima_if(late_from, count)
                    if kt == KT_LEAD and not last:
                        neg_rows(g + 1)
                    values(g, j, kt)
                    if last:
                        if kt % 2 == 0:
                            final_turn(kt // 2)
                        else:
                            final_mm(kt // 2)

            pe.wait_ge(id_ready, 2)
            pe.wait_ge(sub0_done, NT)
            for n, (u, units) in enumerate(tail):
                project(u, f)
                f += 1
                for g, m in units:
                    if m == 0:
                        pe.wait_ge(stack_in[g], per_load)
                    k = g * UNITS + m
                    if k == TAIL_BANK.index(3):
                        pe.wait_ge(x1_added, NT)
                    if k == TAIL_BANK.index(4):
                        pe.wait_ge(x1T_copied, 2 * NT)
                    if k >= len(TAIL_BANK):
                        pe.wait_ge(max_done, k + 1 - len(TAIL_BANK))
                    max_scores(g, m, TAIL_BANK[k % len(TAIL_BANK)])
                if n == TURN:
                    neg_rows(0, 2)
            for u in order[-3:]:
                evacuated(u)
            pe.wait_ge(ones_ready, 3)
            pe.wait_ge(max_done, len(ahead_units))
            pe.wait_ge(m_in, 16)
            scores(0, 0, 0, 0)
            scores(0, 0, 0, 1)
            with pe.Fori(0, NG // BUF) as i:
                for j in range(BUF):
                    group(i * BUF + j, j, i, False)
            group(NG - 1, 0, None, True)
            turn_o(NG)
            final_turn(TB)
            for t in range(TB, NT):
                if t + 1 < NT:
                    final_turn(t + 1)
                final_mm(t)


_INS = ['x', 'ctx_768', 'L0_xattn_w_q', 'L0_xattn_w_k', 'L0_xattn_w_v', 'L0_xattn_w_k_dis', 'L0_xattn_w_v_dis',
        'L0_xattn_w_out', 'L0_xattn_b_out', 'L1_xattn_Wq', 'L1_xattn_Wk', 'L1_xattn_Wv', 'L1_xattn_Wo', 'L1_xattn_bo']
_OUTS = [((2, 512, 320), 'float32')]


def kernel(**inputs):
    import numpy as _np
    import concourse.bacc as _bacc
    from concourse import mybir as _mybir
    from concourse.bass_utils import run_bass_kernel_spmd as _run

    nc = _bacc.Bacc("TRN2", target_bir_lowering=False, num_devices=1)
    arrays, args = {}, []
    for name in _INS:
        a = _np.ascontiguousarray(inputs[name])
        arrays[f"in_{name}_dram"] = a
        args.append(nc.dram_tensor(f"in_{name}_dram", a.shape, _mybir.dt.from_np(a.dtype), kind="ExternalInput").ap())
    for i, (shape, dtype) in enumerate(_OUTS):
        dt = _mybir.dt.from_np(_np.dtype(dtype))
        args.append(nc.dram_tensor(f"out_{i}_dram", shape, dt, kind="ExternalOutput").ap())
    two_layer_cross_attention(nc, *args)
    r = _run(nc, [arrays], core_ids=[0])
    got = tuple(r.results[0][f"out_{i}_dram"] for i in range(len(_OUTS)))
    return got[0]
```

```python
import concourse.bass as bass
import numpy as np
from concourse import mybir
from contextlib import ExitStack

ALU = mybir.AluOpType
ACT = mybir.ActivationFunctionType
AX = mybir.AxisListType
F32 = mybir.dt.float32
BF16 = mybir.dt.bfloat16
F32R = mybir.dt.float32r


def two_layer_cross_attention(nc, x, ctx_768, w_q0, w_k0, w_v0, w_kd0, w_vd0, w_out0, b_out0,
                              w_q1, w_k1, w_v1, w_o1, b_o1, out):
    B, SQ, DM = x.shape
    SK, DC = ctx_768.shape[1:]
    P = 128
    NT = B * SQ // P
    TB = NT // B
    NKT = SK // P
    H0, D0, NS, TOK = 8, 40, 3, 16
    SETS = (0, SK - TOK, TOK)
    KEY0 = NS * TOK
    COL0 = H0 * KEY0
    H1, D1, GH = 20, 16, 4
    GW = GH * D1
    GB = H1 // GH
    NG = B * GB
    CH = [(0, 128), (128, 128), (256, 64)]
    CC = [(0, 128), (128, 64)]
    HC = [(0, 3), (3, 3), (6, 2)]
    NPAIR = [(0, 0), (0, 1), (0, 2), (1, 0), (1, 1), (2, 0)]
    STK = len(NPAIR) * D1
    PB = 3
    BUF = 3
    LEAD = 12
    UNITS = GH * TB * 2
    MAX_BANK = [[0, 1, 0], [1, 0, 7, 1], [0, 7, 1, 0, 7], [1, 0, 7, 1], [0, 7, 1, 0], [1, 0, 1], [0, 1, 7, 0, 1], [7, 0, 1, 7]]
    PLACE = [sum(len(m) for m in MAX_BANK[:kt]) for kt in range(NKT)]
    KT_LEAD = PLACE.index(UNITS - LEAD)
    BANK_AT = sum(MAX_BANK, [])
    assert len(BANK_AT) == UNITS
    FREED_BY = []
    for at in range(UNITS):
        FREED_BY.append(next(d for d in range(1, UNITS + 1) if BANK_AT[at - d] == BANK_AT[at]))
    TAIL_BANK = (0, 1, 3, 4)

    k_parts = nc.dram_tensor("k_parts", [3, B * DM, SK], BF16, kind="Internal").ap()
    q_parts = nc.dram_tensor("q_parts", [3, B * DM, SQ], BF16, kind="Internal").ap()

    with ExitStack() as ctx:
        def sb(name, shape, dt=F32):
            return ctx.enter_context(nc.sbuf_tensor(name, shape, dt))

        def passing(*tensors):
            with ExitStack() as place:
                return [place.enter_context(nc.sbuf_tensor(name, shape, F32)) for name, shape in tensors]

        def sem(name):
            return ctx.enter_context(nc.semaphore(name))

        ident_f = sb("ident_f", [P, P])
        ident_b = sb("ident_b", [P, P], BF16)
        xs = sb("xs", [P, NT, DM])
        (cs,) = passing(("cs", [P, B * NKT, DC]))
        xTl, wq1l = passing(("xTl", [P, 2, B * SQ]), ("wq1l", [P, 3, DM]))
        attn = sb("attn", [P, TB, NG, GW])
        o_raw = sb("o_raw", [P, SQ])
        (x0T,) = passing(("x0T", [P, 3, B * SQ]))
        xT = sb("xT", [P, 3, B * SQ])
        cT = sb("cT", [P, 2, B * SK])
        tokT = sb("tokT", [P, 2, B, NS, TOK])
        wq0 = sb("wq0", [P, 3, DM])
        wk0 = sb("wk0", [P, 2, DM])
        wv0 = sb("wv0", [P, 2, DM])
        wkd0 = sb("wkd0", [P, 2, DM])
        wvd0 = sb("wvd0", [P, 2, DM])
        wout0 = sb("wout0", [P, 3, DM])
        wq1h = sb("wq1h", [P, 3, DM])
        wk1h, wk1l, wv1h, wv1l = passing(*((name, [P, 2, DM]) for name in ("wk1h", "wk1l", "wv1h", "wv1l")))
        oT = sb("oT", [P, 2, 3, P])
        oTl = sb("oTl", [P, 2, 2, P])
        o_turned = sb("o_turned", [P, SQ])
        sb("rest_of_weights", [P, 4 * 2 * DM - 2 * 3 * P - 2 * 2 * P - SQ])
        wo1h = sb("wo1h", [P, 3, DM])
        wo1l = sb("wo1l", [P, 3, DM])
        bias0 = sb("bias0", [P, DM])
        bias1 = sb("bias1", [P, DM])
        mask_k = sb("mask_k", [P, 3 * KEY0])
        mask_v = sb("mask_v", [P, 3 * KEY0])
        U = sb("U", [P, B, 3, DM])
        d0 = sb("d0", [P, 3, COL0])
        max0 = sb("max0", [P, 2, H0 * NS])
        sum0 = sb("sum0", [P, 2, H0 * NS])
        rec0 = sb("rec0", [P, 2, H0 * NS])
        (wo1,) = passing(("wo1", [P, 3, DM]))
        parts = sb("parts", [P, PB, 3, 512], BF16)
        rest = sb("rest", [P, 2, 512])
        x0Tl, wq0h, wq0l = passing(("x0Tl", [P, 2, B * SQ]), ("wq0h", [P, 3, DM]), ("wq0l", [P, 3, DM]))
        _, cTl = passing(("KS_first_buffers", [P, (BUF - 1) * GH * SK // 2]), ("cTl", [P, 1, B * SK]))
        KS = sb("KS", [P, BUF, GH, SK], BF16)
        QS = sb("QS", [P, BUF, GH, SQ], BF16)
        q0T = QS[:, :, :, :].rearrange("p a b c -> p (a b c)").bitcast(F32).rearrange(
            "p (c t) -> p c t", c=3)
        V = sb("V", [P, NG, NKT, GW])
        VS = sb("VS", [P, BUF, NKT, GH, 2 * D1])
        vs = VS[:, :, :, :, :].rearrange("p a k h d -> p (a k h d)")
        wk1, wv1 = (vs[:, n * 2 * DM:(n + 1) * 2 * DM].rearrange("p (c n) -> p c n", c=2) for n in range(2))
        wq1 = vs[:, 4 * DM:7 * DM].rearrange("p (c n) -> p c n", c=3)
        probs = sb("probs", [P, 4, 2, SQ])
        pr = probs[:, :, :, :].rearrange("p a b c -> p (a b c)")
        nk, nv = 3 * B * 3 * KEY0, 3 * B * COL0
        k0bd = pr[:, 0:nk].rearrange("p (c b n) -> p c b n", c=3, b=B)
        v0bd = pr[:, nk:nk + nv].rearrange("p (c b n) -> p c b n", c=3, b=B)
        pT = pr[:, nk + nv:nk + nv + 2 * COL0].rearrange("p (r n) -> p r n", r=2)
        o_rec = sb("o_rec", [P, TB * GH])
        mx = sb("mx", [P, BUF, UNITS])
        neg = sb("neg", [P, TB * GH])
        neg_r = sb("neg_r", [P, TB * GH])
        one = sb("one", [P, TB * GH])
        neg_p = sb("neg_p", [P, 3, GH, TB], BF16)
        mT = sb("mT", [3 * GH, SQ], BF16)
        ps = ctx.enter_context(nc.psum_tensor("ps", [P, 8, 512], F32))

        x_in = [sem(f"x_in{b}") for b in range(B)]
        c_in = [sem(f"c_in{b}") for b in range(B)]
        wq0_in, wkv0_in, wout0_in = sem("wq0_in"), sem("wkv0_in"), sem("wout0_in")
        wq1_in, wk1_in, wv1_in, wo1_in, bias_in = sem("wq1_in"), sem("wk1_in"), sem("wv1_in"), sem("wo1_in"), sem("bias_in")
        id_step, id_ready, mask_step, mask_ready = sem("id_step"), sem("id_ready"), sem("mask_step"), sem("mask_ready")
        zero_ready, ones_ready = sem("zero_ready"), sem("ones_ready")
        xT_mm, x_high, x_low = sem("xT_mm"), sem("x_high"), sem("x_low")
        cT_mm, cT_copied = sem("cT_mm"), sem("cT_copied")
        q0_mm, q0_copied = sem("q0_mm"), sem("q0_copied")
        tok_copied = sem("tok_copied")
        kv0_mm, k0bd_made, v0bd_made = sem("kv0_mm"), sem("k0bd_made"), sem("v0bd_made")
        u_mm, u_copied = sem("u_mm"), sem("u_copied")
        s0_mm, max0_done, sub0_done = sem("s0_mm"), sem("max0_done"), sem("sub0_done")
        exp0_done, sum0_done, rec0_done, norm0_done = sem("exp0_done"), sem("sum0_done"), sem("rec0_done"), sem("norm0_done")
        pT_mm, pT_copied = sem("pT_mm"), sem("pT_copied")
        xb_done, x1_mm, x1_added = sem("xb_done"), sem("x1_mm"), sem("x1_added")
        x1T_mm, x1T_copied, x1b_done = sem("x1T_mm"), sem("x1T_copied"), sem("x1b_done")
        cT_low, x1T_low, w_high, w_low = sem("cT_low"), sem("x1T_low"), sem("w_high"), sem("w_low")
        proj_mm, v_copied = sem("proj_mm"), sem("v_copied")
        hi_done, rest_done, mid_done, lo_done = sem("hi_done"), sem("rest_done"), sem("mid_done"), sem("lo_done")
        stored = [sem(f"stored{k}") for k in range(B * 9)]
        stack_in = [sem(f"stack_in{j}") for j in range(BUF)]
        v_staged, max_mm, max_done = sem("v_staged"), sem("max_mm"), sem("max_done")
        neg_made, neg_step, neg_done, mT_mm, turned_read, m_in = sem("neg_made"), sem("neg_step"), sem("neg_done"), sem("mT_mm"), sem("turned_read"), sem("m_in")
        s_mm, exp_done, pv_mm = sem("s_mm"), sem("exp_done"), sem("pv_mm")
        o_copied, oT_mm, o_rec_done, o_norm = sem("o_copied"), sem("oT_mm"), sem("o_rec_done"), sem("o_norm")
        fT_mm, fT_copied, fT_low, fin_mm, fin_added, out_done = sem("fT_mm"), sem("fT_copied"), sem("fT_low"), sem("fin_mm"), sem("fin_added"), sem("out_done")

        k_units = [[("k", b, c, h) for c in range(3) for h in range(2)] for b in range(B)]
        v_units = [[("v", b, t) for t in range(NKT)] for b in range(B)]
        q_units = [[("q", b, c) for c in range(3)] for b in range(B)]
        STEPS = NT + 4
        k0, k1, v0 = k_units[0], k_units[1], v_units[0]
        plan = [k0[0:1] + v0[0:1], k0[1:2] + v0[1:2], k0[2:3] + v0[2:3], k0[3:4], k0[4:5], k0[5:6],
                [], [], q_units[0], v0[3:4] + k1[0:1], v0[4:5], v0[5:6]]
        assert len(plan) == STEPS
        late = k1[1:3] + v0[6:7] + k1[3:5] + v0[7:8] + k1[5:] + q_units[1] + v_units[1]
        ahead_units = [(0, u) for u in range(UNITS)] + [(1, u) for u in range(LEAD)]
        in_step = {STEPS - 2: 0, STEPS - 1: 3}
        step_units, done = {}, 0
        for step, count in in_step.items():
            step_units[step] = ahead_units[done:done + count]
            done += count
        AHEAD_BANK = [n % 2 for n in range(done)] + [TAIL_BANK[n % len(TAIL_BANK)] for n in range(len(ahead_units) - done)]
        BANK_BEFORE = [max([m for m in range(n) if AHEAD_BANK[m] == AHEAD_BANK[n]], default=None) for n in range(len(ahead_units))]
        tail = []
        for n, u in enumerate(late):
            count = {"k": 2, "q": 4, "v": 4}[u[0]]
            tail.append((u, ahead_units[done:done + count]))
            done += count
        assert done >= len(ahead_units)
        TURN = 2 + next(n for n, (_, units) in enumerate(tail) if (0, UNITS - 1) in units)
        assert TURN < len(tail)
        f_tail = sum(len(step) for step in plan)
        order = [u for step in plan for u in step] + late
        split_no = {u: k for k, u in enumerate(u for u in order if u[0] != "v")}
        PROJ = (5, 6, 7)

        block = ctx.enter_context(nc.Block())

        def group_index(g):
            return g if isinstance(g, int) else g.with_bounds(min_val=0, max_val=NG - 1)

        def xT_bank(u):
            return u if u < 3 else u + 1

        def q0_bank(w):
            return (w + 3 if w < 3 else w + 6) % 4

        split_weights = [(wq0, wq0h, wq0l, 2, wq0_in), (wk1, wk1h, wk1l, 1, wk1_in), (wv1, wv1h, wv1l, 1, wv1_in), (wq1, wq1h, wq1l, 2, wq1_in),
                         (wo1, wo1h, wo1l, 2, wo1_in)]

        def products(w_cols, wh, wl, x_cols, xh, xl):
            whole = wh.shape[1] - 1
            rows = CH[2][1]
            pairs = []
            for k in range(whole):
                pairs += [(wh[:, k, w_cols], xh[:, k, x_cols]), (wh[:, k, w_cols], xl[:, k, x_cols]), (wl[:, k, w_cols], xh[:, k, x_cols])]
            pairs += [(wh[:, whole, w_cols], xh[:, whole, x_cols]), (wl[0:rows, whole, w_cols], xh[0:rows, whole, x_cols])]
            return [(a.bitcast(F32R), b.bitcast(F32R)) for a, b in pairs]

        def outputs_over_sums(g, o):
            dst = attn[:, :, bass.ds(group_index(g), 1), :].rearrange("p q o (h d) -> p q (o h) d", d=D1)
            o = o.rearrange("p (m c) -> p m c", c=2 * D1)[:, :, 0:D1].rearrange("p (q h) d -> p q h d", q=TB)
            return dst, o, o_rec[:, :].rearrange("p (q h) -> p q h", q=TB).unsqueeze(3).to_broadcast([P, TB, GH, D1])

        def load_weight(eng, dst, w, rows, s):
            whole, rest = w.shape[0] // rows, w.shape[0] % rows
            eng.dma_start(dst[0:rows, 0:whole, :], w[0:whole * rows, :].rearrange("(c p) n -> p c n", p=rows)).then_inc(s, 16)
            eng.dma_start(dst[0:rest, whole, :], w[whole * rows:, :]).then_inc(s, 16)

        @block.sync
        def _(sp):
            xv = x.rearrange("b (t p) n -> b p t n", p=P)
            for b in range(B):
                sp.dma_start(xs[:, b * TB:(b + 1) * TB, :], xv[b]).then_inc(x_in[b], 16)
            load_weight(sp, wv0, w_v0, P, wkv0_in)
            load_weight(sp, wvd0, w_vd0, P, wkv0_in)
            load_weight(sp, wout0, w_out0, HC[0][1] * D0, wout0_in)
            for dst, b in ((bias0, b_out0), (bias1, b_o1)):
                sp.dma_start(dst[:, :], b.partition_broadcast(P)).then_inc(bias_in, 16)
            load_weight(sp, wq1, w_q1, P, wq1_in)
            load_weight(sp, wo1, w_o1, P, wo1_in)

            def store(u):
                k = split_no[u]
                sp.wait_ge(lo_done, k + 1)
                r = k % PB
                if u[0] == "q":
                    r0, n = CH[u[2]]
                    dst = q_parts[:, u[1] * DM + r0:u[1] * DM + r0 + n, :].rearrange("a r n -> r a n")
                    sp.dma_start(dst, parts[0:n, r, :, :]).then_inc(stored[k], 16)
                else:
                    r0, n = CH[u[2]]
                    dst = k_parts[:, u[1] * DM + r0:u[1] * DM + r0 + n, u[3] * 512:u[3] * 512 + 512].rearrange("a r n -> r a n")
                    sp.dma_start(dst, parts[0:n, r, :, :]).then_inc(stored[k], 16)

            def load(g, j, stack, scratch, parts_of):
                for n, a in enumerate(parts_of):
                    v = scratch[a, bass.ds(group_index(g) * GW, GW), :].rearrange("(h d) n -> d h n", d=D1)
                    sp.dma_start(stack[n * D1:n * D1 + D1, j, :, :], v).then_inc(stack_in[j], 16)

            def load_k(g, j):
                load(g, j, KS, k_parts, [pk for _, pk in NPAIR])

            def load_q(g, j):
                load(g, j, QS, q_parts, [pq for pq, _ in NPAIR])

            def scratch_written(units):
                for u in units:
                    sp.wait_ge(stored[split_no[u]], 16)

            for u in k_units[0]:
                store(u)
            scratch_written(k_units[0])
            load_k(0, 0)
            load_k(1, 1)
            store(q_units[0][0])
            store(q_units[0][1])
            scratch_written(q_units[0][0:1])
            sp.wait_ge(s0_mm, NT)
            load_q(0, 0)
            for u in q_units[0][2:]:
                store(u)
            for n, u in enumerate(k_units[1] + q_units[1]):
                if n == PB:
                    load_q(1, 1)
                store(u)
            scratch_written(q_units[0][1:] + k_units[1] + q_units[1])

            def max_rows(g, j):
                sp.wait_ge(turned_read, 2 * g if not isinstance(g, int) or g else 1)
                sp.dma_start(QS[STK:STK + 3, j, :, :], mT[:, :]).then_inc(m_in, 16)

            max_rows(0, 0)
            with sp.Fori(0, NG // BUF) as i:
                for j in range(BUF):
                    g = i * BUF + j
                    if j < BUF - 1:
                        sp.wait_ge(s_mm, g * 16 + 1)
                        load_k(g + 2, (j + 2) % BUF)
                        load_q(g + 2, (j + 2) % BUF)
                    else:
                        with sp.If(i < NG // BUF - 1):
                            sp.wait_ge(s_mm, g * 16 + 1)
                            load_k(g + 2, (j + 2) % BUF)
                            load_q(g + 2, (j + 2) % BUF)
                    max_rows(g + 1, (j + 1) % BUF)
            for t in range(NT):
                sp.wait_ge(fin_added, t + 1)
                sp.dma_start(out.rearrange("b (t p) n -> (b t) p n", p=P)[t], xs[:, t, :]).then_inc(out_done, 16)
            sp.wait_ge(out_done, 16 * NT)

        @block.gpsimd
        def _(pool):
            def diagonal(m, done):
                pool.affine_select(out=m, in_=m, compare_op=ALU.not_equal, fill=1.0, base=0,
                                   pattern=[[-1, P]], channel_multiplier=1).then_inc(done, 1)

            pool.memset(ident_f[:, :], 0.0).then_inc(id_step, 1)
            pool.memset(ident_b[:, :], 0.0).then_inc(id_step, 1)
            pool.memset(mask_k[:, :], 1.0).then_inc(mask_step, 1)
            pool.wait_ge(id_step, 2)
            diagonal(ident_f[:, :], id_ready)
            diagonal(ident_b[:, :], id_ready)
            mk = mask_k[:, :].rearrange("p (h k) -> p h k", h=3)
            mv = mask_v[:, :].rearrange("p (h k) -> p h k", h=3)
            pool.wait_ge(mask_step, 1)
            pool.affine_select(out=mk, in_=mk, compare_op=ALU.is_ge, fill=0.0, base=0,
                               pattern=[[-D0, 3], [0, KEY0]], channel_multiplier=1).then_inc(mask_step, 1)
            pool.wait_ge(mask_step, 2)
            pool.affine_select(out=mk, in_=mk, compare_op=ALU.is_ge, fill=0.0, base=D0 - 1,
                               pattern=[[D0, 3], [0, KEY0]], channel_multiplier=-1).then_inc(mask_step, 1)
            pool.wait_ge(mask_step, 3)
            pool.tensor_scalar(mask_v[:, :], mask_k[:, :], 0.5, None, ALU.mult).then_inc(mask_step, 1)
            pool.wait_ge(mask_step, 4)
            pool.tensor_scalar(mv[:, :, TOK:2 * TOK], mk[:, :, TOK:2 * TOK], 1.0, None, ALU.mult).then_inc(mask_ready, 1)
            pool.memset(v0bd, 0.0).then_inc(zero_ready, 1)
            pair_of_ones = float(np.array([0x3F803F80], np.uint32).view(np.float32)[0])
            pool.memset(one[:, :], 1.0).then_inc(ones_ready, 1)
            for b in range(B):
                pool.wait_ge(x_in[b], 16)
                pool.wait_ge(xT_mm, 3 * b + 3)
                pool.wait_ge(bias_in, 32)
                xb = xs[:, b * TB:(b + 1) * TB, :]
                pool.tensor_tensor(xb, xb, bias0[:, :].unsqueeze(1).to_broadcast([P, TB, DM]), ALU.add).then_inc(xb_done, 1)
            pool.wait_ge(w_low, 2 * len(split_weights))
            pool.memset(VS[:, :, :, :, :], 1.0).then_inc(ones_ready, 1)
            pool.wait_ge(q0_mm, 3 * B)
            pool.wait_ge(mask_ready, 1)
            pool.wait_ge(zero_ready, 1)
            pool.wait_ge(xb_done, B)
            pool.wait_ge(ones_ready, 2)
            pool.memset(KS[STK:STK + 3, 0:BUF - 1, :, :].rearrange("p a b c -> p (a b c)").bitcast(F32), pair_of_ones).then_inc(ones_ready, 1)
            pool.wait_ge(ones_ready, 3)

            def split(u):
                if u[0] == "v":
                    return
                k = split_no[u]
                n = CH[u[2]][1]
                pool.wait_ge(mid_done, k + 1)
                pool.tensor_tensor(parts[0:n, k % PB, 2, :], rest[0:n, k % 2, :], parts[0:n, k % PB, 1, :],
                                   ALU.subtract).then_inc(lo_done, 1)

            for s in range(STEPS):
                if 1 <= s <= NT:
                    t = s - 1
                    pool.wait_ge(rec0_done, t + 1)
                    e = d0[:, t % 3, :].rearrange("p (g k) -> p g k", k=TOK)
                    rb = rec0[:, t % 2, :].unsqueeze(2).to_broadcast([P, H0 * NS, TOK])
                    pool.tensor_tensor(e, e, rb, ALU.mult).then_inc(norm0_done, 1)
                for u in plan[s - 1] if s else []:
                    split(u)
                if 4 <= s < NT + 4:
                    t = s - 4
                    pool.wait_ge(x1T_mm, t + 1)
                    pool.tensor_tensor(xs[:, t, :], xs[:, t, :], bias1[:, :], ALU.add).then_inc(x1b_done, 1)
            for u in plan[-1]:
                split(u)

            def stage_v(g, j):
                src = V[:, bass.ds(group_index(g), 1), :, :].rearrange("p o k (h d) -> p (o k) h d", h=GH)
                pool.tensor_copy(VS[:, j, :, :, 0:D1], src).then_inc(v_staged, 1)

            def neg_parts(g):
                pool.wait_ge(neg_made, g + 1)
                pool.wait_ge(mT_mm, g)
                pv = [neg_p[:, a, :, :].rearrange("p h q -> p (h q)") for a in range(3)]
                pool.tensor_tensor(pv[0], neg[:, :], one[:, :], ALU.mult).then_inc(neg_step, 1)
                pool.wait_ge(neg_step, g * 3 + 1)
                pool.tensor_tensor(neg_r[:, :], neg[:, :], pv[0], ALU.subtract).then_inc(neg_step, 1)
                pool.wait_ge(neg_step, g * 3 + 2)
                pool.tensor_tensor(pv[1], neg_r[:, :], one[:, :], ALU.mult).then_inc(neg_step, 1)
                pool.wait_ge(neg_step, g * 3 + 3)
                pool.tensor_tensor(pv[2], neg_r[:, :], pv[1], ALU.subtract).then_inc(neg_done, 1)

            def divide(g):
                pool.wait_ge(o_rec_done, g + 1)
                pool.tensor_tensor(*outputs_over_sums(g, o_turned[:, :]), ALU.mult).then_inc(o_norm, 1)

            pool.wait_ge(ones_ready, 3)
            for u, _ in tail:
                split(u)
            neg_parts(0)
            pool.wait_ge(v_copied, B * NKT)
            stage_v(0, 0)
            pool.wait_ge(v_staged, 1)
            pool.memset(KS[STK:STK + 3, BUF - 1, :, :].rearrange("p b c -> p (b c)").bitcast(F32), pair_of_ones).then_inc(ones_ready, 1)
            pool.wait_ge(ones_ready, 4)
            with pool.Fori(0, NG // BUF) as i:
                for j in range(BUF):
                    g = i * BUF + j
                    pool.wait_ge(s_mm, g * 16 + 1)
                    stage_v(g + 1, (j + 1) % BUF)
                    if j > 0:
                        divide(g - 1)
                    else:
                        with pool.If(i > 0):
                            divide(g - 1)
                    neg_parts(g + 1)
            divide(NG - 2)

        @block.scalar
        def _(act):
            load_weight(act, wq0, w_q0, P, wq0_in)
            cv = ctx_768.rearrange("b (t p) n -> b p t n", p=P)
            for b in range(B):
                act.dma_start(cs[:, b * NKT:(b + 1) * NKT, :], cv[b]).then_inc(c_in[b], 16)
            def copy_q0(b, c0, c1):
                for c in range(c0, c1):
                    w = 3 * b + c
                    n = HC[c][1] * D0
                    act.wait_ge(q0_mm, w + 1)
                    act.copy(q0T[0:n, c, b * SQ:(b + 1) * SQ], ps[0:n, q0_bank(w), :]).then_inc(q0_copied, 1)

            def copy_context(v):
                qd, c = v // 2, v % 2
                n = CC[c][1]
                act.wait_ge(cT_mm, v + 1)
                act.copy(cT[0:n, c, qd * 512:qd * 512 + 512].bitcast(F32R), ps[0:n, 4 + v % 4, :]).then_inc(cT_copied, 1)

            def weight_high(w, high, low, whole, w_in):
                n = CH[2][1]
                act.wait_ge(w_in, 32)
                act.copy(high[:, 0:whole, :].bitcast(F32R), w[:, 0:whole, :]).then_inc(w_high, 1)
                act.copy(high[0:n, whole, :].bitcast(F32R), w[0:n, whole, :]).then_inc(w_high, 1)
                act.copy(high[n:2 * n, whole, :].bitcast(F32R), w[0:n, whole, :]).then_inc(w_high, 1)

            def x_transposed(b):
                for c, (_, n) in enumerate(CH):
                    act.wait_ge(xT_mm, 3 * b + c + 1)
                    act.copy(x0T[0:n, c, b * SQ:(b + 1) * SQ].bitcast(F32R), ps[0:n, xT_bank(3 * b + c), :]).then_inc(x_high, 1)

            x_transposed(0)
            weight_high(*split_weights[0])
            x_transposed(1)
            load_weight(act, wk0, w_k0, P, wkv0_in)
            load_weight(act, wkd0, w_kd0, P, wkv0_in)
            load_weight(act, wk1, w_k1, P, wk1_in)
            load_weight(act, wv1, w_v1, P, wv1_in)
            copy_q0(0, 0, 3)
            for v in range(4):
                copy_context(v)
            copy_q0(1, 0, 1)
            for v in range(4, 8):
                copy_context(v)
            for w in split_weights[1:]:
                weight_high(*w)
            copy_q0(1, 1, 3)
            for y in range(3 * B):
                b, k = y // 3, y % 3
                act.wait_ge(u_mm, y + 1)
                act.copy(U[:, b, k, :], ps[:, 6 + y % 2, 0:DM]).then_inc(u_copied, 1)

            behind = []

            def second_part():
                while behind:
                    k, n = behind.pop(0)
                    act.wait_ge(rest_done, k + 1)
                    act.copy(parts[0:n, k % PB, 1, :], rest[0:n, k % 2, :]).then_inc(mid_done, 1)

            def take(u, f):
                if len(behind) == 2 or f >= f_tail:
                    second_part()
                act.wait_ge(proj_mm, f + 1)
                if u[0] == "v":
                    g0 = u[1] * GB
                    act.copy(V[:, g0:g0 + GB, u[2], :], ps[:, PROJ[f % 3], 0:DM].rearrange("p (g n) -> p g n", g=GB)).then_inc(v_copied, 1)
                    return
                k = split_no[u]
                n = CH[u[2]][1]
                if k >= PB:
                    act.wait_ge(stored[k - PB], 16)
                act.copy(parts[0:n, k % PB, 0, :], ps[0:n, PROJ[f % 3], :]).then_inc(hi_done, 1)
                behind.append((k, n))

            def mT_copy(g, bank=7):
                act.wait_ge(mT_mm, g + 1)
                if not isinstance(g, int):
                    act.wait_ge(m_in, g * 16)
                act.copy(mT[:, :], ps[:, bank, :].bitcast(BF16)[0:3 * GH, 0:SQ]).then_inc(turned_read, 1)

            f = 0
            for s in range(STEPS):
                if s < NT:
                    act.wait_ge(sub0_done, s + 1)
                    act.activation(d0[:, s % 3, :], d0[:, s % 3, :], ACT.Exp, scale=float(D0) ** -0.5).then_inc(exp0_done, 1)
                second_part()
                if 2 <= s < NT + 2:
                    t = s - 2
                    act.wait_ge(pT_mm, t + 1)
                    if t >= 2:
                        act.wait_ge(x1_mm, t - 1)
                    act.copy(pT[:, t % 2, :], ps[:, 2, 0:COL0]).then_inc(pT_copied, 1)
                if 4 <= s < NT + 4:
                    t = s - 4
                    act.wait_ge(x1T_mm, t + 1)
                    act.copy(xT[:, 0:2, t * P:(t + 1) * P].bitcast(F32R), ps[:, 4, 0:2 * P].rearrange("p (c n) -> p c n", c=2)).then_inc(x1T_copied, 1)
                    act.copy(xT[0:64, 2, t * P:(t + 1) * P].bitcast(F32R), ps[0:64, 4, 2 * P:3 * P]).then_inc(x1T_copied, 1)
                for u in plan[s]:
                    take(u, f)
                    f += 1
            for n, (u, _) in enumerate(tail):
                take(u, f)
                f += 1
                if n == TURN:
                    mT_copy(0, 2)

            def exp_pair(g, kt, p):
                n = g * 16 + (2 * kt + p)
                act.wait_ge(s_mm, n + 1)
                if kt >= 2:
                    act.wait_ge(pv_mm, g * NKT + (kt - 1))
                act.activation(probs[:, (2 * kt + p) % 4, :, :], ps[:, 2 + 2 * p:4 + 2 * p, :], ACT.Exp,
                               scale=float(D1) ** -0.5).then_inc(exp_done, 1)

            def copy_o(g):
                act.wait_ge(pv_mm, g * NKT + NKT)
                act.copy(o_raw[:, :], ps[:, 6, :]).then_inc(o_copied, 1)

            def copy_turned(g):
                act.wait_ge(oT_mm, g + 1)
                act.copy(o_turned[:, :], ps[:, 7, :]).then_inc(turned_read, 1)

            def copy_final(t):
                act.wait_ge(fT_mm, t + 1)
                if t >= 2:
                    act.wait_ge(fin_mm, t - 1)
                bk = 0 if t < TB else 2 + t % 2
                act.copy(oT[:, t % 2, 0:2, :].bitcast(F32R), ps[:, bk, 0:2 * P].rearrange("p (c n) -> p c n", c=2)).then_inc(fT_copied, 1)
                act.copy(oT[0:64, t % 2, 2, :].bitcast(F32R), ps[0:64, bk, 2 * P:3 * P]).then_inc(fT_copied, 1)

            def group(g, j, i, last):
                for kt in range(NKT):
                    if kt == 0:
                        if j > 0 or last:
                            copy_o(g - 1)
                        else:
                            with act.If(i > 0):
                                copy_o(g - 1)
                    if kt < NKT - 1:
                        exp_pair(g, kt + 1, 0)
                        exp_pair(g, kt + 1, 1)
                        if kt == 0:
                            if j > 0 or last:
                                copy_turned(g - 1)
                            else:
                                with act.If(i > 0):
                                    copy_turned(g - 1)
                    elif not last:
                        for p in range(2):
                            n = g * 16 + 16 + p
                            act.wait_ge(s_mm, n + 1)
                            act.wait_ge(pv_mm, g * NKT + (NKT - 1))
                            act.activation(probs[:, p, :, :], ps[:, 2 + 2 * p:4 + 2 * p, :], ACT.Exp,
                                           scale=float(D1) ** -0.5).then_inc(exp_done, 1)
                    if kt == KT_LEAD and not last:
                        mT_copy(g + 1)
                    if last and kt % 2 == 0:
                        copy_final(kt // 2)

            exp_pair(0, 0, 0)
            exp_pair(0, 0, 1)
            with act.Fori(0, NG // BUF) as i:
                for j in range(BUF):
                    group(i * BUF + j, j, i, False)
            group(NG - 1, 0, None, True)
            copy_o(NG - 1)
            for t in range(TB, NT):
                copy_final(t)

        @block.vector
        def _(dve):
            def x_transposed(b):
                for c, (_, n) in enumerate(CH):
                    cols = slice(b * SQ, (b + 1) * SQ)
                    low = x0Tl[:, c, cols] if c < 2 else x0T[n:2 * n, 2, cols]
                    dve.wait_ge(x_high, 3 * b + c + 1)
                    dve.tensor_tensor(low.bitcast(F32R), ps[0:n, xT_bank(3 * b + c), :], x0T[0:n, c, cols], ALU.subtract).then_inc(x_low, 1)

            def weight_low(m):
                w, high, low, whole, _ = split_weights[m]
                n = CH[2][1]
                dve.wait_ge(w_high, 3 * m + 3)
                dve.tensor_tensor(low[:, 0:whole, :].bitcast(F32R), w[:, 0:whole, :], high[:, 0:whole, :], ALU.subtract).then_inc(w_low, 1)
                dve.tensor_tensor(low[0:n, whole, :].bitcast(F32R), w[0:n, whole, :], high[0:n, whole, :], ALU.subtract).then_inc(w_low, 1)

            x_transposed(0)
            weight_low(0)
            x_transposed(1)
            for v in range(8):
                qd, c = v // 2, v % 2
                n = CC[c][1]
                b, first = qd // 2, qd % 2 * 512
                bank = ps[0:n, 4 + v % 4, :]
                dve.wait_ge(cT_copied, v + 1)
                for st, t0 in enumerate(SETS):
                    if first <= t0 < first + 512:
                        dve.tensor_copy(tokT[0:n, c, b, st, :], bank[:, t0 - first:t0 - first + TOK]).then_inc(tok_copied, 1)
                low = cTl[:, 0, qd * 512:qd * 512 + 512] if c == 0 else cT[n:2 * n, 1, qd * 512:qd * 512 + 512]
                dve.tensor_tensor(low.bitcast(F32R), bank, cT[0:n, c, qd * 512:qd * 512 + 512], ALU.subtract).then_inc(cT_low, 1)
            for m in range(1, len(split_weights)):
                weight_low(m)
            dve.wait_ge(mask_ready, 1)
            for kv, (bank, made, mask) in enumerate(((4, k0bd_made, mask_k), (5, v0bd_made, mask_v))):
                dve.wait_ge(kv0_mm, kv + 1)
                if kv:
                    dve.wait_ge(zero_ready, 1)
                for c, (h0, nh) in enumerate(HC):
                    n = nh * D0
                    src = ps[0:n, bank, c * B * KEY0:(c + 1) * B * KEY0].rearrange("p (b k) -> p b k", b=B)
                    dst = v0bd[0:n, c, :, h0 * KEY0:(h0 + nh) * KEY0] if kv else k0bd[0:n, c, :, 0:nh * KEY0]
                    dve.tensor_tensor(dst.rearrange("p b (h k) -> p b h k", h=nh),
                                      src.unsqueeze(2).to_broadcast([n, B, nh, KEY0]),
                                      mask[0:n, 0:nh * KEY0].rearrange("p (h k) -> p h k", h=nh).unsqueeze(1).to_broadcast([n, B, nh, KEY0]),
                                      ALU.mult).then_inc(made, 1)

            def leave_rest(u, f):
                if u[0] == "v":
                    return
                k = split_no[u]
                n = CH[u[2]][1]
                dve.wait_ge(hi_done, k + 1)
                if k >= 2:
                    dve.wait_ge(lo_done, k - 1)
                dve.tensor_tensor(rest[0:n, k % 2, :], ps[0:n, PROJ[f % 3], :], parts[0:n, k % PB, 0, :],
                                  ALU.subtract).then_inc(rest_done, 1)

            def maximum(g, j, u, bank):
                n = g * UNITS + u
                dve.wait_ge(max_mm, n + 1)
                dve.tensor_reduce(mx[:, j, u:u + 1], ps[:, bank, :], AX.X, ALU.max).then_inc(max_done, 1)

            def negate(g, j):
                dve.wait_ge(max_done, g * UNITS + UNITS)
                dve.wait_ge(neg_done, g)
                dve.tensor_reduce(neg[:, :], mx[:, j, :].rearrange("p (m h) -> p m h", h=2), AX.X, ALU.max,
                                  negate=True).then_inc(neg_made, 1)

            f = 0
            for s in range(STEPS):
                if s < NT:
                    sc = ps[:, s % 2, 0:COL0].rearrange("p (g k) -> p g k", k=TOK)
                    dve.wait_ge(s0_mm, s + 1)
                    dve.tensor_reduce(max0[:, s % 2, :], sc, AX.X, ALU.max).then_inc(max0_done, 1)
                    dve.wait_ge(max0_done, s + 1)
                    if s >= 3:
                        dve.wait_ge(pT_mm, s - 2)
                    dve.tensor_tensor(d0[:, s % 3, :].rearrange("p (g k) -> p g k", k=TOK), sc,
                                      max0[:, s % 2, :].unsqueeze(2).to_broadcast([P, H0 * NS, TOK]),
                                      ALU.subtract).then_inc(sub0_done, 1)
                if 1 <= s <= NT:
                    t = s - 1
                    dve.wait_ge(exp0_done, t + 1)
                    dve.tensor_reduce(sum0[:, t % 2, :], d0[:, t % 3, :].rearrange("p (g k) -> p g k", k=TOK),
                                      AX.X, ALU.add).then_inc(sum0_done, 1)
                    dve.wait_ge(sum0_done, t + 1)
                    if t >= 2:
                        dve.wait_ge(norm0_done, t - 1)
                    dve.reciprocal(rec0[:, t % 2, :], sum0[:, t % 2, :]).then_inc(rec0_done, 1)
                for u in (plan[0], [])[s] if s < 2 else plan[s - 1]:
                    leave_rest(u, f)
                    f += 1
                if 3 <= s < NT + 3:
                    t = s - 3
                    dve.wait_ge(x1_mm, t + 1)
                    dve.wait_ge(xb_done, t // TB + 1)
                    dve.tensor_tensor(xs[:, t, :], ps[:, 3, 0:DM], xs[:, t, :], ALU.add).then_inc(x1_added, 1)
                if 4 <= s < NT + 4:
                    t = s - 4
                    cols = slice(t * P, (t + 1) * P)
                    dve.wait_ge(x1T_copied, 2 * t + 2)
                    dve.tensor_tensor(xTl[:, :, cols].bitcast(F32R), ps[:, 4, 0:2 * P].rearrange("p (c n) -> p c n", c=2),
                                      xT[:, 0:2, cols], ALU.subtract).then_inc(x1T_low, 1)
                    dve.tensor_tensor(xT[64:P, 2, cols].bitcast(F32R), ps[0:64, 4, 2 * P:3 * P], xT[0:64, 2, cols],
                                      ALU.subtract).then_inc(x1T_low, 1)
                for g, m in step_units.get(s, []):
                    maximum(g, g, m, AHEAD_BANK[m])
            for u in plan[-1]:
                leave_rest(u, f)
                f += 1

            def invert_sums(g, o, read):
                dve.wait_ge(*read)
                dve.reciprocal(o_rec[:, :], o.rearrange("p (m c) -> p m c", c=2 * D1)[:, :, D1]).then_inc(o_rec_done, 1)

            def group(g, j, i, last):
                for kt in range(NKT):
                    if kt == 1:
                        if j > 0 or last:
                            invert_sums(g - 1, o_turned[:, :], (turned_read, 2 * g + 1))
                        else:
                            with dve.If(i > 0):
                                invert_sums(g - 1, o_turned[:, :], (turned_read, 2 * g + 1))
                    if last:
                        continue
                    ahead = j + (2 if kt >= KT_LEAD else 1)

                    def maxima():
                        for n, bank in enumerate(MAX_BANK[kt]):
                            maximum(g + ahead - j, ahead % BUF, (PLACE[kt] + n + LEAD) % UNITS, bank)

                    if kt < KT_LEAD or j < BUF - 1:
                        maxima()
                    else:
                        with dve.If(i < NG // BUF - 1):
                            maxima()
                    if kt == KT_LEAD - 1:
                        negate(g + 1, (j + 1) % BUF)

            for u, units in tail:
                leave_rest(u, f)
                f += 1
                for g, m in units:
                    maximum(g, g, m, AHEAD_BANK[g * UNITS + m])
                    if (g, m) == (0, UNITS - 1):
                        negate(0, 0)
            with dve.Fori(0, NG // BUF) as i:
                for j in range(BUF):
                    group(i * BUF + j, j, i, False)

            def final_low(t):
                bank = ps[:, 0 if t < TB else 2 + t % 2, :]
                dve.wait_ge(fT_copied, 2 * t + 2)
                dve.tensor_tensor(oTl[:, t % 2, :, :].bitcast(F32R), bank[:, 0:2 * P].rearrange("p (c n) -> p c n", c=2),
                                  oT[:, t % 2, 0:2, :], ALU.subtract).then_inc(fT_low, 1)
                dve.tensor_tensor(oT[64:P, t % 2, 2, :].bitcast(F32R), bank[0:64, 2 * P:3 * P], oT[0:64, t % 2, 2, :],
                                  ALU.subtract).then_inc(fT_low, 1)

            def final(t):
                dve.wait_ge(fin_mm, t + 1)
                dve.wait_ge(x1b_done, t + 1)
                bk = 1 if t < TB else 4 + t % 2
                dve.tensor_tensor(xs[:, t, :], ps[:, bk, 0:DM], xs[:, t, :], ALU.add).then_inc(fin_added, 1)

            group(NG - 1, 0, None, True)
            for t in range(TB):
                final_low(t)
                final(t)
            g, o = NG - 1, ps[:, 7, :]
            dve.wait_ge(o_norm, g)
            invert_sums(g, o, (oT_mm, NG))
            dve.wait_ge(o_rec_done, NG)
            dve.tensor_tensor(*outputs_over_sums(g, o), ALU.mult).then_inc(o_norm, 1)
            final_low(TB)
            for t in range(TB, NT):
                if t + 1 < NT:
                    final_low(t + 1)
                final(t)

        @block.tensor
        def _(pe):
            def mm_chain(dst, pairs, s=None):
                for n, (l, r) in enumerate(pairs):
                    m = pe.matmul(dst, l, r, start=(n == 0), stop=(n == len(pairs) - 1))
                if s is not None:
                    m.then_inc(s, 1)
                return m

            pe.wait_ge(id_ready, 1)
            def turn_x(b):
                pe.wait_ge(x_in[b], 16)
                for c, (r0, n) in enumerate(CH):
                    u = 3 * b + c
                    for k in range(TB):
                        m = pe.transpose(ps[0:n, xT_bank(u), k * P:(k + 1) * P], xs[:, b * TB + k, r0:r0 + n], ident_f[:, :])
                    m.then_inc(xT_mm, 1)

            def queries0(b, c0, c1):
                pe.wait_ge(w_low, 2)
                pe.wait_ge(x_low, 3 * b + 3)
                if b:
                    pe.wait_ge(q0_copied, 3)
                for c in range(c0, c1):
                    h0, nh = HC[c]
                    mm_chain(ps[0:nh * D0, q0_bank(3 * b + c), :],
                             products(slice(h0 * D0, (h0 + nh) * D0), wq0h, wq0l, slice(b * SQ, (b + 1) * SQ), x0T, x0Tl), q0_mm)

            turn_x(0)
            turn_x(1)
            queries0(0, 0, 3)
            pe.wait_ge(x_low, 3 * B)

            def turn_context(v):
                qd, c = v // 2, v % 2
                r0, n = CC[c]
                pe.wait_ge(c_in[qd // 2], 16)
                if v >= 4:
                    pe.wait_ge(cT_low, v - 3)
                for k in range(4):
                    m = pe.transpose(ps[0:n, 4 + v % 4, k * P:(k + 1) * P], cs[:, qd * 4 + k, r0:r0 + n], ident_f[:, :])
                m.then_inc(cT_mm, 1)

            for v in range(4):
                turn_context(v)
            queries0(1, 0, 1)
            for v in range(4, 8):
                turn_context(v)
            queries0(1, 1, 3)
            pe.wait_ge(tok_copied, 2 * B * NS)
            pe.wait_ge(wkv0_in, 16 * 8)
            for kv, (dis, anat) in enumerate(((wkd0, wk0), (wvd0, wv0))):
                for c, (h0, nh) in enumerate(HC):
                    dst = ps[0:nh * D0, 4 + kv, c * B * KEY0:(c + 1) * B * KEY0].rearrange("p (b s k) -> p b s k", b=B, s=NS)
                    for w, s0, s1 in ((dis, 0, 2), (anat, 2, 3)):
                        m = mm_chain(dst[:, :, s0:s1, :],
                                     [(w[0:n, k, h0 * D0:(h0 + nh) * D0], tokT[0:n, k, :, s0:s1, :]) for k, (_, n) in enumerate(CC)])
                m.then_inc(kv0_mm, 1)
            pe.wait_ge(v0bd_made, 3)
            pe.wait_ge(wout0_in, 32)
            for y in range(3 * B):
                b, k = y // 3, y % 3
                if y >= 2:
                    pe.wait_ge(u_copied, y - 1)
                cs_in = [c for c, (h0, nh) in enumerate(HC) if h0 * KEY0 < (k + 1) * P and (h0 + nh) * KEY0 > k * P]
                mm_chain(ps[:, 6 + y % 2, 0:DM],
                         [(v0bd[0:HC[c][1] * D0, c, b, k * P:(k + 1) * P], wout0[0:HC[c][1] * D0, c, :]) for c in cs_in], u_mm)
            pe.wait_ge(q0_copied, 3 * B)
            pe.wait_ge(k0bd_made, 3)

            def evacuated(u):
                if u[0] == "v":
                    pe.wait_ge(v_copied, u[1] * NKT + u[2] + 1)
                else:
                    pe.wait_ge(rest_done, split_no[u] + 1)

            def project(u, f):
                bank = PROJ[f % 3]
                pe.wait_ge(w_low, 2 * len(split_weights))
                pe.wait_ge(cT_low, 8)
                if f >= 3:
                    evacuated(order[f - 3])
                if u[0] == "k":
                    _, b, c, h = u
                    r0, n = CH[c]
                    keys = slice(b * SK + h * 512, b * SK + h * 512 + 512)
                    mm_chain(ps[0:n, bank, :], products(slice(r0, r0 + n), wk1h, wk1l, keys, cT, cTl), proj_mm)
                elif u[0] == "v":
                    _, b, t = u
                    pairs = products(slice(0, DM), wv1h, wv1l, slice(b * SK + t * P, b * SK + (t + 1) * P), cT, cTl)
                    mm_chain(ps[:, bank, 0:DM], [(x_part, w_part) for w_part, x_part in pairs], proj_mm)
                else:
                    _, b, c = u
                    r0, n = CH[c]
                    pe.wait_ge(x1T_low, 2 * TB * (b + 1))
                    mm_chain(ps[0:n, bank, :], products(slice(r0, r0 + n), wq1h, wq1l, slice(b * SQ, (b + 1) * SQ), xT, xTl), proj_mm)

            def max_scores(j, u, bank):
                h, qt, half = u // (2 * TB), u // 2 % TB, u % 2
                pe.matmul(ps[:, bank, :], QS[0:STK, j, h, qt * P:(qt + 1) * P], KS[0:STK, j, h, half * 512:half * 512 + 512],
                          start=True, stop=True).then_inc(max_mm, 1)

            per_load = 16 * 2 * len(NPAIR)

            def max_ahead(units):
                for g, m in units:
                    k = g * UNITS + m
                    if k == 0:
                        pe.wait_ge(sub0_done, NT)
                    if m == 0:
                        pe.wait_ge(stack_in[g], per_load)
                    if k == AHEAD_BANK.index(3):
                        pe.wait_ge(x1_added, NT)
                    if k == AHEAD_BANK.index(4):
                        pe.wait_ge(x1T_low, 2 * NT)
                    if BANK_BEFORE[k] is not None:
                        pe.wait_ge(max_done, BANK_BEFORE[k] + 1)
                    max_scores(g, m, AHEAD_BANK[k])

            f = 0
            for s in range(STEPS):
                if s < NT:
                    if s >= 2:
                        pe.wait_ge(sub0_done, s - 1)
                    for c, (h0, nh) in enumerate(HC):
                        n = nh * D0
                        m = pe.matmul(ps[:, s % 2, h0 * KEY0:(h0 + nh) * KEY0], q0T[0:n, c, s * P:(s + 1) * P],
                                      k0bd[0:n, c, s // TB, 0:nh * KEY0], start=True, stop=True)
                    m.then_inc(s0_mm, 1)
                if 2 <= s < NT + 2:
                    t = s - 2
                    pe.wait_ge(norm0_done, t + 1)
                    if t >= 1:
                        pe.wait_ge(pT_copied, t)
                    for k in range(3):
                        m = pe.transpose(ps[:, 2, k * P:(k + 1) * P], d0[:, t % 3, k * P:(k + 1) * P], ident_f[:, :])
                    m.then_inc(pT_mm, 1)
                if 3 <= s < NT + 3:
                    t = s - 3
                    pe.wait_ge(pT_copied, t + 1)
                    if t >= 1:
                        pe.wait_ge(x1_added, t)
                    mm_chain(ps[:, 3, 0:DM], [(pT[:, t % 2, k * P:(k + 1) * P], U[:, t // TB, k, :]) for k in range(3)], x1_mm)
                if 4 <= s < NT + 4:
                    t = s - 4
                    pe.wait_ge(x1_added, t + 1)
                    if t >= 1:
                        pe.wait_ge(x1T_low, 2 * t)
                    for c, (r0, n) in enumerate(CH):
                        m = pe.transpose(ps[0:n, 4, c * P:(c + 1) * P], xs[:, t, r0:r0 + n], ident_f[:, :])
                    m.then_inc(x1T_mm, 1)
                if s == 0:
                    pe.wait_ge(u_copied, 3 * B)
                for u in plan[s]:
                    project(u, f)
                    f += 1
                max_ahead(step_units.get(s, []))

            def neg_rows(g, bank=7):
                pe.wait_ge(neg_done, g + 1)
                for qt in range(TB):
                    m = pe.transpose(ps[:, bank, :].bitcast(BF16)[0:3 * GH, qt * P:(qt + 1) * P], neg_p[:, :, :, qt], ident_b[:, :])
                m.then_inc(mT_mm, 1)

            def scores(g, j, kt, p):
                n = g * 16 + (2 * kt + p)
                if not isinstance(n, int) or n >= 2:
                    pe.wait_ge(exp_done, n - 1)
                for h in (2 * p, 2 * p + 1):
                    m = pe.matmul(ps[:, 2 + h, :], KS[0:STK + 3, j, h, kt * P:(kt + 1) * P], QS[0:STK + 3, j, h, :],
                                  start=True, stop=True)
                m.then_inc(s_mm, 1)

            def values(g, j, kt):
                pe.wait_ge(exp_done, g * 16 + (2 * kt + 2))
                for h in range(GH):
                    m = pe.matmul(ps[2 * D1 * h:2 * D1 * (h + 1), 6, :], VS[:, j, kt, h, :],
                                  probs[:, (2 * kt + h // 2) % 4, h % 2, :], start=(kt == 0), stop=(kt == NKT - 1))
                m.then_inc(pv_mm, 1)

            def turn_o(g):
                pe.wait_ge(o_copied, g)
                if isinstance(g, int) and g == NG:
                    pe.wait_ge(turned_read, 2 * g - 1)
                elif isinstance(g, int):
                    pe.wait_ge(turned_read, 2 * g)
                else:
                    pe.wait_ge(turned_read, 2 * g)
                    pe.wait_ge(max_done, g * UNITS + UNITS + LEAD)
                for qt in range(TB):
                    m = pe.transpose(ps[:, 7, qt * P:(qt + 1) * P], o_raw[:, qt * P:(qt + 1) * P], ident_f[:, :])
                m.then_inc(oT_mm, 1)

            def final_turn(t):
                b, qt = t // TB, t % TB
                if t < TB:
                    pe.wait_ge(o_norm, GB)
                    if t == 0:
                        pe.wait_ge(max_done, NG * UNITS)
                    else:
                        pe.wait_ge(fT_low, 2 * t)
                else:
                    pe.wait_ge(o_norm, NG)
                    pe.wait_ge(fT_low, 2 * (t - 1))
                bk = 0 if t < TB else 2 + t % 2
                for c in range(2):
                    pe.transpose(ps[:, bk, c * P:(c + 1) * P], attn[:, qt, b * GB + 2 * c:b * GB + 2 * c + 2, :].rearrange("p g n -> p (g n)"), ident_f[:, :])
                pe.transpose(ps[0:64, bk, 2 * P:3 * P], attn[:, qt, b * GB + 4, :], ident_f[:, :]).then_inc(fT_mm, 1)

            def final_mm(t):
                pe.wait_ge(fT_low, 2 * t + 2)
                if t < TB:
                    if t >= 1:
                        pe.wait_ge(fin_added, t)
                else:
                    pe.wait_ge(fin_added, t - 1)
                bk = 1 if t < TB else 4 + t % 2
                mm_chain(ps[:, bk, 0:DM], [(x_part, w_part) for w_part, x_part in
                                                products(slice(0, DM), wo1h, wo1l, slice(0, P), oT[:, t % 2, :, :], oTl[:, t % 2, :, :])], fin_mm)

            def group(g, j, i, last):
                for kt in range(NKT):
                    ahead = j + (2 if kt >= KT_LEAD else 1)
                    gg, jj = g + ahead - j, ahead % BUF

                    def maxima(n0, n1):
                        if last or n0 == n1:
                            return
                        if n0 == 0 and kt in (0, KT_LEAD):
                            pe.wait_ge(stack_in[jj], (i + ahead // BUF + 1) * per_load)
                        for at in range(PLACE[kt] + n0, PLACE[kt] + n1):
                            u = (at + LEAD) % UNITS
                            pe.wait_ge(max_done, gg * UNITS + u + 1 - FREED_BY[at])
                            if at == BANK_AT.index(7):
                                pe.wait_ge(turned_read, 2 * g + 1)
                            if BANK_AT[at] == 7 and kt == KT_LEAD + 1:
                                pe.wait_ge(turned_read, 2 * g + 2)
                            max_scores(jj, u, BANK_AT[at])

                    def maxima_if(n0, n1):
                        if last or n0 == n1 or kt < KT_LEAD or j < BUF - 1:
                            maxima(n0, n1)
                        else:
                            with pe.If(i < NG // BUF - 1):
                                maxima(n0, n1)

                    maxima_if(0, 2)
                    if kt < NKT - 1:
                        scores(g, j, kt + 1, 0)
                    elif not last:
                        pe.wait_ge(m_in, g * 16 + 32)
                        if j == 1:
                            pe.wait_ge(ones_ready, 4)
                        scores(g + 1, (j + 1) % BUF, 0, 0)
                    count = len(MAX_BANK[kt])
                    late_from = min(3, count - 1)
                    maxima_if(2, late_from)
                    if kt < NKT - 1:
                        scores(g, j, kt + 1, 1)
                    elif not last:
                        scores(g + 1, (j + 1) % BUF, 0, 1)
                    if kt == 0:
                        if j > 0 or last:
                            turn_o(g)
                        else:
                            with pe.If(i > 0):
                                turn_o(g)
                        pe.wait_ge(v_staged, g + 1)
                    maxima_if(late_from, count)
                    if kt == KT_LEAD and not last:
                        neg_rows(g + 1)
                    values(g, j, kt)
                    if last:
                        if kt % 2 == 0:
                            final_turn(kt // 2)
                        else:
                            final_mm(kt // 2)

            pe.wait_ge(id_ready, 2)
            for n, (u, units) in enumerate(tail):
                project(u, f)
                f += 1
                max_ahead(units)
                if n == TURN:
                    neg_rows(0, 2)
            for u in order[-3:]:
                evacuated(u)
            pe.wait_ge(ones_ready, 3)
            pe.wait_ge(max_done, len(ahead_units))
            pe.wait_ge(m_in, 16)
            scores(0, 0, 0, 0)
            scores(0, 0, 0, 1)
            with pe.Fori(0, NG // BUF) as i:
                for j in range(BUF):
                    group(i * BUF + j, j, i, False)
            group(NG - 1, 0, None, True)
            turn_o(NG)
            final_turn(TB)
            for t in range(TB, NT):
                if t + 1 < NT:
                    final_turn(t + 1)
                final_mm(t)


_INS = ['x', 'ctx_768', 'L0_xattn_w_q', 'L0_xattn_w_k', 'L0_xattn_w_v', 'L0_xattn_w_k_dis', 'L0_xattn_w_v_dis',
        'L0_xattn_w_out', 'L0_xattn_b_out', 'L1_xattn_Wq', 'L1_xattn_Wk', 'L1_xattn_Wv', 'L1_xattn_Wo', 'L1_xattn_bo']
_OUTS = [((2, 512, 320), 'float32')]


def kernel(**inputs):
    import numpy as _np
    import concourse.bacc as _bacc
    from concourse import mybir as _mybir
    from concourse.bass_utils import run_bass_kernel_spmd as _run

    nc = _bacc.Bacc("TRN2", target_bir_lowering=False, num_devices=1)
    arrays, args = {}, []
    for name in _INS:
        a = _np.ascontiguousarray(inputs[name])
        arrays[f"in_{name}_dram"] = a
        args.append(nc.dram_tensor(f"in_{name}_dram", a.shape, _mybir.dt.from_np(a.dtype), kind="ExternalInput").ap())
    for i, (shape, dtype) in enumerate(_OUTS):
        dt = _mybir.dt.from_np(_np.dtype(dtype))
        args.append(nc.dram_tensor(f"out_{i}_dram", shape, dt, kind="ExternalOutput").ap())
    two_layer_cross_attention(nc, *args)
    r = _run(nc, [arrays], core_ids=[0])
    got = tuple(r.results[0][f"out_{i}_dram"] for i in range(len(_OUTS)))
    return got[0]
```
